# Optimizing a Trainium2 kernel written in Bass

```python
import numpy as np
import jax
import jax.numpy as jnp

def _softmax(x, axis=-1):
    return jax.nn.softmax(x, axis=axis)

def _gelu(x):
    return jax.nn.gelu(x, approximate=True)

def _silu(x):
    return jax.nn.silu(x)

def _sigmoid(x):
    return jax.nn.sigmoid(x)

def _layernorm(x, axis=-1, eps=1e-05):
    m = jnp.mean(x, axis=axis, keepdims=True)
    v = jnp.var(x, axis=axis, keepdims=True)
    return (x - m) / jnp.sqrt(v + eps)

def _scatter_add(tgt, idx, src, axis=0):
    return tgt.at[idx].add(src)

def _segment_sum(src, seg, n):
    return jax.ops.segment_sum(src, seg, n)
kernel_name = 'mk_prb_d1_jaxref_r8_e1c778'

def setup_inputs(seed: int=0):
    np.random.seed(seed)
    _w = jnp.asarray

    def _L0_attn_setup():
        import math
        import jax, jax.numpy as jnp
        import numpy as np
        B, L, HID = (2, 256, 256)
        H = 16
        D = HID // H
        EPS = 1e-06
        ROPE_BASE = 10000.0
        BETA_MIN, BETA_MAX = (0.8, 0.9995)

        def _rope_cache(seq_len, dim):
            half = dim // 2
            inv_freq = 1.0 / ROPE_BASE ** (jnp.arange(half, dtype=jnp.float32) / float(half))
            t = jnp.arange(seq_len, dtype=jnp.float32)
            freqs = t[:, None] * inv_freq[None, :]
            return (jnp.cos(freqs), jnp.sin(freqs))

        def _apply_rope(x, cos, sin):
            half = x.shape[-1] // 2
            xe, xo = (x[..., :half], x[..., half:])
            c = cos[None, None]
            s = sin[None, None]
            return jnp.concatenate([xe * c - xo * s, xe * s + xo * c], axis=-1)

        def _deltanet(x, Wq, Wk, Wv, Wg, bg, Wo, bo):
            Bb, Ll, _ = x.shape
            split = lambda t: t.reshape(Bb, Ll, H, D).transpose(0, 2, 1, 3)
            q = split(x @ Wq)
            k = split(x @ Wk)
            v = split(x @ Wv)
            cos, sin = _rope_cache(Ll, D)
            q = _apply_rope(q, cos, sin)
            k = _apply_rope(k, cos, sin)
            beta = jax.nn.sigmoid(x @ Wg + bg)
            beta = jnp.clip(beta, BETA_MIN, BETA_MAX).transpose(0, 2, 1)
            phi_q = jax.nn.elu(q) + 1.0
            phi_k = jax.nn.elu(k) + 1.0
            pq = phi_q.transpose(2, 0, 1, 3)
            pk = phi_k.transpose(2, 0, 1, 3)
            vt = v.transpose(2, 0, 1, 3)
            bt = beta.transpose(2, 0, 1)
            S0 = jnp.zeros((Bb, H, D, D), jnp.float32)
            z0 = jnp.zeros((Bb, H, D), jnp.float32)

            def step(carry, inp):
                S, z = carry
                pq_t, pk_t, v_t, b_t = inp
                S = S * b_t[..., None, None] + pk_t[..., :, None] * v_t[..., None, :]
                z = z * b_t[..., None] + pk_t
                numer = jnp.einsum('bhd,bhde->bhe', pq_t, S)
                denom = jnp.sum(pq_t * z, axis=-1, keepdims=True) + EPS
                return ((S, z), numer / denom)
            (_, _), y = jax.lax.scan(step, (S0, z0), (pq, pk, vt, bt))
            y = y.transpose(1, 0, 2, 3).reshape(Bb, Ll, HID)
            return y @ Wo + bo
        key = jax.random.key(seed)
        ks = jax.random.split(key, 6)
        sc = 1.0 / math.sqrt(HID)
        return {'x': jax.random.normal(ks[0], (B, L, HID), jnp.float32), 'Wq': jax.random.normal(ks[1], (HID, HID), jnp.float32) * sc, 'Wk': jax.random.normal(ks[2], (HID, HID), jnp.float32) * sc, 'Wv': jax.random.normal(ks[3], (HID, HID), jnp.float32) * sc, 'Wg': jax.random.normal(ks[4], (HID, H), jnp.float32) * sc, 'bg': jnp.full((H,), math.log(0.98 / (1.0 - 0.98)), jnp.float32), 'Wo': jax.random.normal(ks[5], (HID, HID), jnp.float32) * sc, 'bo': jnp.zeros((HID,), jnp.float32)}
    _L0_attn_in = _L0_attn_setup()

    def _L0_ffn_setup():
        import jax, jax.numpy as jnp
        import numpy as np
        HIDDEN = 256
        INTER = 1024
        RETRIEVAL = 128
        NUM_EXPERTS = 512
        NUM_KEYS = 64
        TOP_K = 8
        B, S = (4, 256)
        key = jax.random.key(seed)
        ks = jax.random.split(key, 8)
        sc = 0.02
        return {'hidden_states': jax.random.normal(ks[0], (B, S, HIDDEN), jnp.float32), 'W_q': jax.random.normal(ks[1], (HIDDEN, RETRIEVAL), jnp.float32) * sc, 'keys': jax.random.normal(ks[2], (2, RETRIEVAL // 2, NUM_KEYS), jnp.float32) * sc, 'down_embed': jax.random.normal(ks[3], (NUM_EXPERTS, HIDDEN), jnp.float32) * sc, 'up_embed': jax.random.normal(ks[4], (NUM_EXPERTS, HIDDEN), jnp.float32) * sc, 'gate_w': jax.random.normal(ks[5], (HIDDEN, INTER), jnp.float32) * sc, 'up_w': jax.random.normal(ks[6], (HIDDEN, INTER), jnp.float32) * sc, 'down_w': jax.random.normal(ks[7], (INTER, HIDDEN), jnp.float32) * sc}
    _L0_ffn_in = _L0_ffn_setup()
    _d = {'L0_attn_x': _L0_attn_in['x'], 'L0_attn_Wq': _L0_attn_in['Wq'], 'L0_attn_Wk': _L0_attn_in['Wk'], 'L0_attn_Wv': _L0_attn_in['Wv'], 'L0_attn_Wg': _L0_attn_in['Wg'], 'L0_attn_bg': _L0_attn_in['bg'], 'L0_attn_Wo': _L0_attn_in['Wo'], 'L0_attn_bo': _L0_attn_in['bo'], 'L0_ffn_W_q': _L0_ffn_in['W_q'], 'L0_ffn_keys': _L0_ffn_in['keys'], 'L0_ffn_down_embed': _L0_ffn_in['down_embed'], 'L0_ffn_up_embed': _L0_ffn_in['up_embed'], 'L0_ffn_gate_w': _L0_ffn_in['gate_w'], 'L0_ffn_up_w': _L0_ffn_in['up_w'], 'L0_ffn_down_w': _L0_ffn_in['down_w']}
    _x0 = _d['L0_attn_x']
    _d['L0_attn_x'] = jax.random.normal(jax.random.fold_in(jax.random.key(seed), 1), (1, 1024, 256), dtype=_x0.dtype)
    del _x0
    return _d

def reference(L0_attn_x, L0_attn_Wq, L0_attn_Wk, L0_attn_Wv, L0_attn_Wg, L0_attn_bg, L0_attn_Wo, L0_attn_bo, L0_ffn_W_q, L0_ffn_keys, L0_ffn_down_embed, L0_ffn_up_embed, L0_ffn_gate_w, L0_ffn_up_w, L0_ffn_down_w):

    def _L0_attn_ref(x, Wq, Wk, Wv, Wg, bg, Wo, bo):
        import math
        import jax, jax.numpy as jnp
        import numpy as np
        B, L, HID = (2, 256, 256)
        H = 16
        D = HID // H
        EPS = 1e-06
        ROPE_BASE = 10000.0
        BETA_MIN, BETA_MAX = (0.8, 0.9995)

        def _rope_cache(seq_len, dim):
            half = dim // 2
            inv_freq = 1.0 / ROPE_BASE ** (jnp.arange(half, dtype=jnp.float32) / float(half))
            t = jnp.arange(seq_len, dtype=jnp.float32)
            freqs = t[:, None] * inv_freq[None, :]
            return (jnp.cos(freqs), jnp.sin(freqs))

        def _apply_rope(x, cos, sin):
            half = x.shape[-1] // 2
            xe, xo = (x[..., :half], x[..., half:])
            c = cos[None, None]
            s = sin[None, None]
            return jnp.concatenate([xe * c - xo * s, xe * s + xo * c], axis=-1)

        def _deltanet(x, Wq, Wk, Wv, Wg, bg, Wo, bo):
            Bb, Ll, _ = x.shape
            split = lambda t: t.reshape(Bb, Ll, H, D).transpose(0, 2, 1, 3)
            q = split(x @ Wq)
            k = split(x @ Wk)
            v = split(x @ Wv)
            cos, sin = _rope_cache(Ll, D)
            q = _apply_rope(q, cos, sin)
            k = _apply_rope(k, cos, sin)
            beta = jax.nn.sigmoid(x @ Wg + bg)
            beta = jnp.clip(beta, BETA_MIN, BETA_MAX).transpose(0, 2, 1)
            phi_q = jax.nn.elu(q) + 1.0
            phi_k = jax.nn.elu(k) + 1.0
            pq = phi_q.transpose(2, 0, 1, 3)
            pk = phi_k.transpose(2, 0, 1, 3)
            vt = v.transpose(2, 0, 1, 3)
            bt = beta.transpose(2, 0, 1)
            S0 = jnp.zeros((Bb, H, D, D), jnp.float32)
            z0 = jnp.zeros((Bb, H, D), jnp.float32)

            def step(carry, inp):
                S, z = carry
                pq_t, pk_t, v_t, b_t = inp
                S = S * b_t[..., None, None] + pk_t[..., :, None] * v_t[..., None, :]
                z = z * b_t[..., None] + pk_t
                numer = jnp.einsum('bhd,bhde->bhe', pq_t, S)
                denom = jnp.sum(pq_t * z, axis=-1, keepdims=True) + EPS
                return ((S, z), numer / denom)
            (_, _), y = jax.lax.scan(step, (S0, z0), (pq, pk, vt, bt))
            y = y.transpose(1, 0, 2, 3).reshape(Bb, Ll, HID)
            return y @ Wo + bo
        return _deltanet(x, Wq, Wk, Wv, Wg, bg, Wo, bo)

    def _L0_ffn_ref(hidden_states, W_q, keys, down_embed, up_embed, gate_w, up_w, down_w):
        import jax, jax.numpy as jnp
        import numpy as np
        HIDDEN = 256
        INTER = 1024
        RETRIEVAL = 128
        NUM_EXPERTS = 512
        NUM_KEYS = 64
        TOP_K = 8
        B, S = (4, 256)
        b, s, h = hidden_states.shape
        n = b * s
        queries = (hidden_states @ W_q).reshape(2, n, RETRIEVAL // 2)
        routing = jnp.einsum('tnd,tdk->tnk', queries, keys)
        scores2, idx2 = jax.lax.top_k(routing, TOP_K)
        sx, sy = (scores2[0], scores2[1])
        ix, iy = (idx2[0], idx2[1])
        all_scores = (sx[:, :, None] + sy[:, None, :]).reshape(n, TOP_K * TOP_K)
        all_idx = (ix[:, :, None] * NUM_KEYS + iy[:, None, :]).reshape(n, TOP_K * TOP_K)
        scores, pk = jax.lax.top_k(all_scores, TOP_K)
        indices = jnp.take_along_axis(all_idx, pk, axis=-1)
        de = down_embed[indices]
        ue = up_embed[indices]
        x = hidden_states.reshape(n, h)
        ew = jnp.einsum('nh,nkh->nk', x, de)
        ew = jax.nn.silu(ew) * jax.nn.softmax(scores, axis=-1)
        experts_states = jnp.einsum('nk,nkh->nh', ew, ue).reshape(b, s, h)
        mlp = jax.nn.silu(x @ gate_w) * (x @ up_w) @ down_w
        return mlp.reshape(b, s, h) + experts_states
    x = L0_attn_x
    xn = _layernorm(x, axis=-1)
    x = x + _L0_attn_ref(xn, L0_attn_Wq, L0_attn_Wk, L0_attn_Wv, L0_attn_Wg, L0_attn_bg, L0_attn_Wo, L0_attn_bo) + _L0_ffn_ref(xn, L0_ffn_W_q, L0_ffn_keys, L0_ffn_down_embed, L0_ffn_up_embed, L0_ffn_gate_w, L0_ffn_up_w, L0_ffn_down_w)
    return x

_drawn_inputs = setup_inputs


def setup_inputs(seed=0):
    import zlib

    import numpy as np

    out = dict(_drawn_inputs(seed))
    spreads = {'L0_attn_bg': (3.891820192337036, 0.2), 'L0_attn_bo': (0.0, 0.1)}
    factors = {'L0_attn_Wq': 3.138,
     'L0_attn_Wg': 2.992,
     'L0_ffn_W_q': 8.0,
     'L0_ffn_keys': 8.0,
     'L0_ffn_down_embed': 8.0,
     'L0_ffn_up_embed': 8.0}
    for name, (base, spread) in spreads.items():
        noise = np.random.default_rng([zlib.crc32(name.encode()), seed]).standard_normal(out[name].shape)
        drawn = base * np.exp(spread * noise) if base else spread * noise
        out[name] = jnp.asarray(drawn.astype(out[name].dtype))
    for name, factor in factors.items():
        out[name] = (out[name] * factor).astype(out[name].dtype)
    return out
```

```python
from contextlib import ExitStack

import concourse.bass as bass
from concourse import mybir

F32 = mybir.dt.float32
BF16 = mybir.dt.bfloat16
U32 = mybir.dt.uint32
ALU = mybir.AluOpType
ACT = mybir.ActivationFunctionType
AX = mybir.AxisListType

P = 128
N_TOK = 1024
HID = 256
KC = HID // P
NT = N_TOK // P
NG = NT
HEADS = 16
D = HID // HEADS
E1 = D + 1
HG = 2
HPG = HEADS // HG
INTER = 1024
MC = INTER // P
NEXP = 512
EC = NEXP // P
NKEY = 64
TOPK = 8
NXI = NEXP // NKEY
EPS_DEN = 1e-6
EPS_LN = 1e-5
BETA_MIN, BETA_MAX = 0.8, 0.9995
MARK = -3.0e38

CONST_PARTS = [("ident", P), ("causal", P), ("headblock", HPG * E1), ("cos", NT * D), ("sin", NT * D),
               ("parity", 2), ("keyno", NKEY * TOPK), ("rankweight", TOPK), ("xno", NXI * TOPK),
               ("chunkcol", NT), ("headrows", HG * P)]


def const_columns():
    at, out = 0, {}
    for name, n in CONST_PARTS:
        out[name] = (at, at + n)
        at += n
    return out, at


def build(nc, x, Wq, Wk, Wv, Wg, bg, Wo, bo, W_qr, keys, down_embed, up_embed, gate_w, up_w, down_w, consts, out):
    cols, n_const = const_columns()
    x_g = x.rearrange("a (t p j) d -> p (a t) (j d)", p=P, j=2)
    out_g = out.rearrange("a (t p j) d -> p (a t) (j d)", p=P, j=2)

    def rows(w):
        return w.rearrange("(k p) n -> p k n", p=P)

    with ExitStack() as ctx:
        def sb(name, shape, dt=F32):
            return ctx.enter_context(nc.sbuf_tensor(name, shape, dt))

        def sem(name):
            return ctx.enter_context(nc.semaphore(name))

        bank = [ctx.enter_context(nc.psum_tensor(f"bank{i}", [P, 512], F32)) for i in range(8)]

        cst = sb("cst", [P, n_const])

        def con(name):
            a, b = cols[name]
            return cst[:, a:b]

        ident = con("ident")
        x_sb = sb("x_sb", [P, NG, HID])
        xn = sb("xn", [P, 2, HID])
        stats = sb("stats", [P, NG, 6])
        mv = sb("mv", [P, NG, 2])
        std = sb("std", [P, NG])
        rstd = sb("rstd", [P, NG])
        xnT = sb("xnT", [P, KC, N_TOK])
        early = sb("early", [P, 2048])
        wqk_sb = early[:, 0:1024].rearrange("p (k n) -> p k n", k=KC)
        wv_sb = early[:, 1024:1536].rearrange("p (k n) -> p k n", k=KC)
        wqr_sb = early[:, 1536:1792].rearrange("p (k n) -> p k n", k=KC)
        keys_sb = early[:, 1792:2048].rearrange("p (k n) -> p k n", k=2)
        sc = early[:, :].rearrange("p (j r n) -> p j r n", j=4, r=4)
        wg_sb = sb("wg_sb", [P, KC, HEADS])
        wo_sb = sb("wo_sb", [P, KC, HID])
        gate_sb = sb("gate_sb", [P, KC, INTER])
        up_sb = sb("up_sb", [P, KC, INTER])
        down_sb = sb("down_sb", [P, MC, HID])
        de_sb = sb("de_sb", [P, EC, HID])
        sil = de_sb[:, :, :].rearrange("p (u e) n -> p u (e n)", u=2)
        deT = sb("deT", [P, KC, NEXP])
        ue_sb = sb("ue_sb", [P, EC, HID])
        bo_sb = sb("bo_sb", [P, HID])
        bg_sb = sb("bg_sb", [P, HEADS])

        qrT = sb("qrT", [P, N_TOK])
        route = sb("route", [P, 2, NG, NKEY])
        top = sb("top", [P, 2, NG, TOPK])
        topi = sb("topi", [P, 2, NG, TOPK], U32)
        xi = sb("xi", [P, NG, TOPK])
        yi = sb("yi", [P, NG, TOPK], BF16)
        pair = sb("pair", [P, NG, TOPK * TOPK])
        pair8 = sb("pair8", [P, NG, TOPK])
        marked = sb("marked", [P, NG, TOPK * TOPK])
        chosen = sb("chosen", [P, NG, TOPK * TOPK])
        pexp = sb("pexp", [P, NG, TOPK * TOPK])
        rowcount = sb("rowcount", [P, NG, TOPK])
        rowsum = sb("rowsum", [P, NG, TOPK])
        total = sb("total", [P, NG])
        rtotal = sb("rtotal", [P, NG])
        xmatch = sb("xmatch", [P, NG, NXI, TOPK])
        xcount = sb("xcount", [P, NG, NXI])
        xlimit = sb("xlimit", [P, NG, NXI])
        beyond = sb("beyond", [P, NG, TOPK])
        beyond1 = sb("beyond1", [P, NG])
        xw = sb("xw", [P, NG, NXI])
        yw = sb("yw", [P, NG, NKEY])
        keyno = sb("keyno", [P, NKEY, TOPK], BF16)
        rankweight = sb("rankweight", [P, TOPK], BF16)
        hT = sb("hT", [P, EC, N_TOK])
        ymatch = hT[:, 0:2, :].rearrange("p e n -> p (e n)").bitcast(BF16).rearrange("p (g j b) -> p g j b", g=NG, b=TOPK)
        yt4 = hT[:, 2, :].bitcast(BF16).rearrange("p (g j b) -> p g j b", g=NG, b=4)
        yrank = sb("yrank", [P, NG, NKEY])
        prob = sb("prob", [P, NG, NXI, NKEY])

        zb = sb("zb", [P, NT, HEADS])
        beta = sb("beta", [P, NT * HEADS])
        betaT = sb("betaT", [P, P])
        ones = sb("ones", [P, P])
        decT = sb("decT", [P, P])
        rdecT = sb("rdecT", [P, P])
        rdec = sb("rdec", [P, NT, HEADS])
        endcol = sb("endcol", [P, NT])
        enddec = sb("enddec", [P, HG, NT])
        actT = sb("actT", [P, MC, N_TOK])
        ropeA, ropeB, rot, relu, ex = (actT[:, i, :].rearrange("p (b n) -> p b n", b=2) for i in range(5))
        phi = sb("phi", [P, NT, 2 * HID])
        v1 = sb("v1", [P, NT, HEADS, E1])
        qT = sb("qT", [P, HG, P])
        kz = sb("kz", [P, 2, HG, P])
        upd = sb("upd", [P, HG, HPG * E1])
        state = sb("state", [P, HG, HPG * E1])
        den = sb("den", [P, HEADS])
        rden = sb("rden", [P, HEADS])
        y = sb("y", [P, HEADS, D])
        yT = sb("yT", [P, HG, N_TOK])

        fin = gate_sb[:, :, :].rearrange("p k n -> p (k n)").rearrange("p (g n) -> p g n", g=NG)
        coefT = up_sb[:, 0, :].rearrange("p (e b n) -> p e b n", e=EC, b=2)

        names = """x0_in x1_in x2_in x3_in consts_in route_in keyx_in qkv_in gate_in up_in embed_in late_in bias_in
            keys_zero xn_ready stat_ready aggr_ready std_in std_ready rstd_ready xnT_done xnT_ready qr_done qrT_ready route_done route_ready
            z_done zb_ready zexp_ready zden_ready zrec_ready beta_ready betaT_done betaT_ready ones_ready decT_ready rdecT_ready
            rdec_done rdec_ready endcol_ready enddec_done enddec_ready
            qk_done v_done v_ready ropeAB_ready rot_ready relu_ready ex_ready phi_ready kp_ready v1_ones
            deT_done deT_ready
            top_ready topi_ready xi_ready pair_ready pair8_ready marked_ready chosen_ready pdif_ready pexp_ready
            wdif_ready xw_exp yw_exp psel_ready rowcount_ready rowsum_ready total_ready rtotal_ready
            bf_consts ymatch_ready yrank_steps xmatch_ready xmatchc_ready xcount_ready xlimit_ready beyond_ready beyond1_ready
            xw_ready prob0_ready prob1_ready prob_ready beyond2_ready
            qkT_done qT_ready kz_ready s_done sc_ready u_done upd_ready state_ready y_done den_ready rden_ready
            y_ready yT_done yT_ready
            gate_done up_done silu_ready mlp_ready h_done h_ready pT_done coef_ready fin_done xb_ready fin_ready out_done""".split()
        S = {n: sem(n) for n in names}

        block = ctx.enter_context(nc.Block())

        def fill(n):
            return bank[n % 3]

        def group_cols(g):
            T, j = divmod(g, 2)
            return slice(T * 2 * P + j, (T + 1) * 2 * P - 1 + j, 2)

        @block.sync
        def _(sp):
            for T in range(NG // 2):
                sp.dma_start(x_sb[:, 2 * T:2 * T + 2, :].rearrange("p j d -> p (j d)"), x_g[:, T, :]).then_inc(S[f"x{T}_in"], 16)
            sp.dma_start(wqr_sb, rows(W_qr)).then_inc(S["route_in"], 16)
            sp.wait_ge(S["keys_zero"], 1)
            for half in range(2):
                for j in range(2):
                    sp.dma_start(keys_sb[64 * j:64 * j + 64, half, NKEY * j:NKEY * j + NKEY], keys[half]).then_inc(S["keyx_in"], 16)
            sp.dma_start(wg_sb[:], rows(Wg)).then_inc(S["qkv_in"], 16)
            sp.dma_start(wqk_sb[:, :, 0:HID], rows(Wq)).then_inc(S["qkv_in"], 16)
            sp.dma_start(wqk_sb[:, :, HID:2 * HID], rows(Wk)).then_inc(S["qkv_in"], 16)
            sp.dma_start(wv_sb, rows(Wv)).then_inc(S["qkv_in"], 16)
            sp.dma_start(gate_sb[:], rows(gate_w)).then_inc(S["gate_in"], 16)
            sp.dma_start(up_sb[:], rows(up_w)).then_inc(S["up_in"], 16)
            sp.dma_start(de_sb[:], rows(down_embed)).then_inc(S["embed_in"], 16)
            sp.dma_start(down_sb[:], rows(down_w)).then_inc(S["late_in"], 16)
            sp.dma_start(ue_sb[:], rows(up_embed)).then_inc(S["late_in"], 16)
            sp.dma_start(wo_sb[:], rows(Wo)).then_inc(S["late_in"], 16)
            for T in range(NG // 2):
                sp.wait_ge(S["fin_ready"], 2 * T + 2)
                sp.dma_start(out_g[:, T, :], fin[:, 2 * T:2 * T + 2, :].rearrange("p j d -> p (j d)")).then_inc(S["out_done"], 16)
            sp.wait_ge(S["out_done"], 16 * (NG // 2))

        @block.gpsimd
        def _(pool):
            g = nc.gpsimd
            g.memset(keys_sb, 0.0).then_inc(S["keys_zero"], 1)
            g.memset(v1[:], 1.0).then_inc(S["v1_ones"], 1)
            g.memset(ones[:], 1.0).then_inc(S["ones_ready"], 1)

            def key_scale(t):
                nc.gpsimd.wait_ge(S["phi_ready"], t + 1)
                if t == 0:
                    nc.gpsimd.wait_ge(S["rdec_ready"], 1)
                kk = phi[:, t, HID:2 * HID].rearrange("p (h d) -> p h d", d=D)
                nc.gpsimd.tensor_tensor(kk, kk, rdec[:, t].unsqueeze(2).broadcast_to([P, HEADS, D]), ALU.mult).then_inc(S["kp_ready"], 1)

            for t in range(NT):
                pool.wait_ge(S["ropeAB_ready"], 2 * t + 2)
                if t >= 2:
                    pool.wait_ge(S["phi_ready"], t - 1)
                    pool.wait_ge(S["ex_ready"], t - 1)
                o, a, b = (z[:, t % 2, :].rearrange("p (h s d) -> p h s d", s=2, d=D // 2) for z in (rot, ropeA, ropeB))
                for s in range(2):
                    g.tensor_tensor(o[:, :, s, :], a[:, :, s, :], b[:, :, 1 - s, :], ALU.add).then_inc(S["rot_ready"], 1)
                if t >= 5:
                    key_scale(2 * t - 10)
                    key_scale(2 * t - 9)
            key_scale(NT - 2)
            key_scale(NT - 1)

            pool.wait_ge(S["bias_in"], 32)
            pool.wait_ge(S["xn_ready"], NG)
            g.tensor_tensor(x_sb[:], x_sb[:], bo_sb[:].unsqueeze(1).broadcast_to([P, NG, HID]), ALU.add).then_inc(S["xb_ready"], 1)

            pool.wait_ge(S["top_ready"], 2 * NG)
            g.tensor_tensor(pair[:].rearrange("p g (a b) -> p g a b", b=TOPK),
                            top[:, 0].unsqueeze(3).broadcast_to([P, NG, TOPK, TOPK]),
                            top[:, 1].unsqueeze(2).broadcast_to([P, NG, TOPK, TOPK]), ALU.add).then_inc(S["pair_ready"], 1)
            g.tensor_tensor(xw[:], route[:, 0, :, 0:NXI], top[:, 0, :, 0:1].broadcast_to([P, NG, NXI]), ALU.subtract).then_inc(S["wdif_ready"], 1)
            g.tensor_tensor(yw[:], route[:, 1], top[:, 1, :, 0:1].broadcast_to([P, NG, NKEY]), ALU.subtract).then_inc(S["wdif_ready"], 1)
            pool.wait_ge(S["pair_ready"], 1)
            g.tensor_tensor(pexp[:], pair[:], pair[:, :, 0:1].broadcast_to([P, NG, TOPK * TOPK]), ALU.subtract).then_inc(S["pdif_ready"], 1)
            pool.wait_ge(S["chosen_ready"], 1)
            pool.wait_ge(S["pexp_ready"], 1)
            g.tensor_tensor(pexp[:], pexp[:], chosen[:], ALU.mult).then_inc(S["psel_ready"], 1)
            pool.wait_ge(S["xmatch_ready"], 1)
            pool.wait_ge(S["rowcount_ready"], 1)
            g.tensor_tensor(xmatch[:], xmatch[:], rowcount[:].unsqueeze(2).broadcast_to([P, NG, NXI, TOPK]), ALU.mult).then_inc(S["xmatchc_ready"], 1)
            pool.wait_ge(S["xw_exp"], 1)
            pool.wait_ge(S["rtotal_ready"], 1)
            g.tensor_tensor(xw[:], xw[:], rtotal[:].unsqueeze(2).broadcast_to([P, NG, NXI]), ALU.mult).then_inc(S["xw_ready"], 1)
            pool.wait_ge(S["yw_exp"], 1)
            for q in range(NG):
                pool.wait_ge(S["prob0_ready"], q + 1)
                g.tensor_tensor(prob[:, q], prob[:, q], yw[:, q].unsqueeze(1).broadcast_to([P, NXI, NKEY]), ALU.mult).then_inc(S["prob1_ready"], 1)
                pool.wait_ge(S["prob1_ready"], q + 1)
                if q == 0:
                    pool.wait_ge(S["xw_ready"], 1)
                g.tensor_tensor(prob[:, q], prob[:, q], xw[:, q].unsqueeze(2).broadcast_to([P, NXI, NKEY]), ALU.mult).then_inc(S["prob_ready"], 1)

        @block.scalar
        def _(act):
            a = nc.scalar
            a.dma_start(cst[:], consts).then_inc(S["consts_in"], 16)
            a.dma_start(bo_sb[:], bo.rearrange("(a n) -> a n", a=1).broadcast_to([P, HID])).then_inc(S["bias_in"], 16)
            a.dma_start(bg_sb[:], bg.rearrange("(a n) -> a n", a=1).broadcast_to([P, HEADS])).then_inc(S["bias_in"], 16)
            for T in range(NG // 2):
                act.wait_ge(S["std_in"], T + 1)
                a.activation(std[:, 2 * T:2 * T + 2], std[:, 2 * T:2 * T + 2], ACT.Sqrt).then_inc(S["std_ready"], 1)
            for g in range(NG):
                act.wait_ge(S["xnT_done"], g + 1)
                a.activation(xnT[:, :, group_cols(g)], bank[g % 2][:, 0:2 * P].rearrange("p (k n) -> p k n", k=KC), ACT.Copy).then_inc(S["xnT_ready"], 1)
            for half in range(2):
                act.wait_ge(S["route_done"], half + 1)
                a.activation(route[:, half].rearrange("p g n -> p (g n)"), bank[4 + half][:], ACT.Copy).then_inc(S["route_ready"], 1)
            act.wait_ge(S["zb_ready"], 1)
            a.activation(zb[:], zb[:], ACT.Exp, scale=-1.0).then_inc(S["zexp_ready"], 1)
            act.wait_ge(S["v1_ones"], 1)
            for t in range(NT + 1):
                if t < NT:
                    act.wait_ge(S["v_done"], t + 1)
                    a.activation(v1[:, t, :, 0:D], bank[2 + t % 2][:, 0:HID].rearrange("p (h d) -> p h d", d=D), ACT.Copy).then_inc(S["v_ready"], 1)
                if t >= 1:
                    act.wait_ge(S["rot_ready"], 2 * t)
                    if t >= 3:
                        act.wait_ge(S["phi_ready"], t - 2)
                    a.activation(relu[:, (t - 1) % 2], rot[:, (t - 1) % 2], ACT.Relu).then_inc(S["relu_ready"], 1)
                    a.activation(ex[:, (t - 1) % 2], rot[:, (t - 1) % 2], ACT.Exp).then_inc(S["ex_ready"], 1)
            for k in range(KC):
                act.wait_ge(S["deT_done"], k + 1)
                a.activation(deT[:, k], bank[4 + k][:], ACT.Copy).then_inc(S["deT_ready"], 1)
            act.wait_ge(S["wdif_ready"], 2)
            a.activation(xw[:], xw[:], ACT.Exp).then_inc(S["xw_exp"], 1)
            a.activation(yw[:], yw[:], ACT.Exp).then_inc(S["yw_exp"], 1)
            act.wait_ge(S["pdif_ready"], 1)
            a.activation(pexp[:], pexp[:], ACT.Exp).then_inc(S["pexp_ready"], 1)

            def silu(u):
                act.wait_ge(S["gate_done"], u + 1)
                if u >= 2:
                    act.wait_ge(S["mlp_ready"], u - 1)
                a.activation(sil[:, u % 2], fill(2 * u)[:], ACT.Silu).then_inc(S["silu_ready"], 1)

            def copy_yT(c):
                act.wait_ge(S["yT_done"], c + 1)
                a.activation(yT[:, :, c * P:(c + 1) * P], bank[7][:, 0:256].rearrange("p (k n) -> p k n", k=HG), ACT.Copy).then_inc(S["yT_ready"], 1)

            for c in range(NT):
                silu(2 * c)
                act.wait_ge(S["qkT_done"], c + 1)
                if c >= 1:
                    act.wait_ge(S["s_done"], 4 * c)
                    act.wait_ge(S["y_done"], c)
                a.activation(qT[:], bank[5][:, 0:2 * P].rearrange("p (k n) -> p k n", k=HG), ACT.Copy).then_inc(S["qT_ready"], 1)
                for par in range(2):
                    a.activation(kz[:, par], bank[5][:, 2 * P:4 * P].rearrange("p (k n) -> p k n", k=HG), ACT.Copy,
                                 scale=con("parity")[:, par:par + 1]).then_inc(S["kz_ready"], 1)
                if c >= 1:
                    copy_yT(c - 1)
                silu(2 * c + 1)
            for v in range(2 * EC):
                e, half = divmod(v, 2)
                act.wait_ge(S["h_done"], v + 1)
                if v == 0:
                    act.wait_ge(S["yrank_steps"], 4)
                a.activation(hT[:, e, half * 512:half * 512 + 512], fill(4 * MC + v)[:], ACT.Silu).then_inc(S["h_ready"], 1)
                if v == 0:
                    copy_yT(NT - 1)

        @block.tensor
        def _(pe):
            t_ = nc.tensor
            pe.wait_ge(S["consts_in"], 16)
            for g in range(NG):
                pe.wait_ge(S["xn_ready"], g + 1)
                if g >= 2:
                    pe.wait_ge(S["xnT_ready"], g - 1)
                for k in range(KC):
                    mm = t_.transpose(bank[g % 2][:, k * P:(k + 1) * P], xn[:, g % 2, k * P:(k + 1) * P], ident)
                mm.then_inc(S["xnT_done"], 1)
            pe.wait_ge(S["route_in"], 16)
            for half in range(2):
                pe.wait_ge(S["xnT_ready"], 4 * half + 4)
                for k in range(KC):
                    mm = t_.matmul(bank[2 + half][:], wqr_sb[:, k, :], xnT[:, k, half * 512:half * 512 + 512], start=k == 0, stop=k == KC - 1)
                mm.then_inc(S["qr_done"], 1)
            pe.wait_ge(S["keyx_in"], 64)
            for half in range(2):
                pe.wait_ge(S["qrT_ready"], half + 1)
                for i in range(4):
                    c = (4 * half + i) * P
                    mm = t_.matmul(bank[4 + half][:, i * P:(i + 1) * P], qrT[:, c:c + P], keys_sb[:, half, :], start=True, stop=True)
                mm.then_inc(S["route_done"], 1)
            pe.wait_ge(S["qkv_in"], 64)
            for t in range(NT):
                for k in range(KC):
                    mm = t_.matmul(bank[6][:, t * HEADS:(t + 1) * HEADS], xnT[:, k, t * P:(t + 1) * P], wg_sb[:, k, :], start=k == 0, stop=k == KC - 1)
            mm.then_inc(S["z_done"], 1)
            for t in range(NT):
                pe.wait_ge(S["xnT_ready"], NG) if t == 0 else pe.wait_ge(S["ropeAB_ready"], 2 * (t - 1)) if t >= 2 else None
                for k in range(KC):
                    mm = t_.matmul(bank[t % 2][:], xnT[:, k, t * P:(t + 1) * P], wqk_sb[:, k, :], start=k == 0, stop=k == KC - 1)
                mm.then_inc(S["qk_done"], 1)
                if t >= 2:
                    pe.wait_ge(S["v_ready"], t - 1)
                for k in range(KC):
                    mm = t_.matmul(bank[2 + t % 2][:, 0:HID], xnT[:, k, t * P:(t + 1) * P], wv_sb[:, k, :], start=k == 0, stop=k == KC - 1)
                mm.then_inc(S["v_done"], 1)
                if t == 1:
                    pe.wait_ge(S["beta_ready"], 1)
                    t_.transpose(bank[7][:, 0:P], beta[:], ident).then_inc(S["betaT_done"], 1)
                if t == 3:
                    pe.wait_ge(S["rdecT_ready"], 1)
                    t_.transpose(bank[7][:, P:2 * P], rdecT[:], ident).then_inc(S["rdec_done"], 1)
                    pe.wait_ge(S["endcol_ready"], 1)
                    for hg in range(HG):
                        mm = t_.matmul(bank[6][:, hg * NT:(hg + 1) * NT], con("headrows")[:, hg * P:(hg + 1) * P], endcol[:], start=True, stop=True)
                    mm.then_inc(S["enddec_done"], 1)
            pe.wait_ge(S["embed_in"], 16)
            for k in range(KC):
                pe.wait_ge(S["route_ready"], k + 1)
                for e in range(EC):
                    mm = t_.transpose(bank[4 + k][:, e * P:(e + 1) * P], de_sb[:, e, k * P:(k + 1) * P], ident)
                mm.then_inc(S["deT_done"], 1)

            pe.wait_ge(S["gate_in"], 16)
            pe.wait_ge(S["up_in"], 16)

            def gate(u):
                m, half = divmod(u, 2)
                if u == 0:
                    pe.wait_ge(S["ropeAB_ready"], 2 * NT)
                    pe.wait_ge(S["v_ready"], NT)
                if u >= 2:
                    pe.wait_ge(S["mlp_ready"], u - 1)
                for k in range(KC):
                    mm = t_.matmul(fill(2 * u)[:], gate_sb[:, k, m * P:(m + 1) * P], xnT[:, k, half * 512:half * 512 + 512], start=k == 0, stop=k == KC - 1)
                mm.then_inc(S["gate_done"], 1)

            def up(u):
                m, half = divmod(u, 2)
                if u >= 1:
                    pe.wait_ge(S["silu_ready"], u)
                for k in range(KC):
                    mm = t_.matmul(fill(2 * u + 1)[:], up_sb[:, k, m * P:(m + 1) * P], xnT[:, k, half * 512:half * 512 + 512], start=k == 0, stop=k == KC - 1)
                mm.then_inc(S["up_done"], 1)

            def qk_transposes(c):
                pe.wait_ge(S["kp_ready"], c + 1)
                if c == 0:
                    pe.wait_ge(S["deT_ready"], KC)
                if c >= 1:
                    pe.wait_ge(S["kz_ready"], 2 * c)
                for k in range(4):
                    mm = t_.transpose(bank[5][:, k * P:(k + 1) * P], phi[:, c, k * P:(k + 1) * P], ident)
                mm.then_inc(S["qkT_done"], 1)

            def scores(c, first):
                if first == 0:
                    pe.wait_ge(S["kz_ready"], 2 * c + 2)
                for j in (first, first + 1):
                    b = bank[3 + j % 2]
                    n = 4 * c + j
                    if n >= 2:
                        pe.wait_ge(S["sc_ready"], n - 1)
                    for r in range(4):
                        hg, par = divmod(r, 2)
                        mm = t_.matmul(b[:, r * P:(r + 1) * P], kz[32 * j:32 * j + 32, par, hg, :], qT[32 * j:32 * j + 32, hg, :], start=True, stop=True)
                    mm.then_inc(S["s_done"], 1)

            def chunk_update(c):
                if c >= 1:
                    pe.wait_ge(S["yT_ready"], c)
                for hg in range(HG):
                    mm = t_.matmul(bank[7][:, hg * HPG * E1:(hg + 1) * HPG * E1], phi[:, c, HID + hg * P:HID + (hg + 1) * P], v1[:, c, hg * HPG:(hg + 1) * HPG, :].rearrange("p h e -> p (h e)"), start=True, stop=True)
                mm.then_inc(S["u_done"], 1)

            def outputs(c):
                first = True
                if c >= 1:
                    pe.wait_ge(S["state_ready"], 2 * c)
                    for hg in range(HG):
                        t_.matmul(bank[6][:, hg * HPG * E1:(hg + 1) * HPG * E1], qT[:, hg, :], state[:, hg, :], start=first, stop=False, skip_group_check=True)
                        first = False
                pe.wait_ge(S["sc_ready"], 4 * c + 4)
                for j in range(4):
                    for r in range(4):
                        h = HPG * (r // 2) + 2 * j + r % 2
                        mm = t_.matmul(bank[6][:, h * E1:(h + 1) * E1], sc[:, j, r, :], v1[:, c, h, :], start=first, stop=(j == 3 and r == 3), skip_group_check=True)
                        first = False
                mm.then_inc(S["y_done"], 1)

            def y_transposes(c):
                pe.wait_ge(S["y_ready"], c + 1)
                pe.wait_ge(S["upd_ready"], 2 * min(c + 1, NT - 1))
                for k in range(HG):
                    mm = t_.transpose(bank[7][:, k * P:(k + 1) * P], y[:, k * HPG:(k + 1) * HPG, :].rearrange("p h d -> p (h d)"), ident)
                mm.then_inc(S["yT_done"], 1)

            for c in range(NT):
                gate(2 * c)
                qk_transposes(c)
                if c >= 1:
                    y_transposes(c - 1)
                up(2 * c)
                scores(c, 0)
                gate(2 * c + 1)
                scores(c, 2)
                if c == 0:
                    pe.wait_ge(S["rdec_ready"], 1)
                    pe.wait_ge(S["enddec_ready"], 1)
                    pe.wait_ge(S["zb_ready"], 1)
                if c < NT - 1:
                    chunk_update(c)
                up(2 * c + 1)
                if c >= 1:
                    pe.wait_ge(S["y_ready"], c)
                outputs(c)

            for v in range(2 * EC):
                e, half = divmod(v, 2)
                if v == 0:
                    pe.wait_ge(S["mlp_ready"], 2 * MC - 1)
                    pe.wait_ge(S["silu_ready"], 2 * MC)
                elif v == 2:
                    pe.wait_ge(S["mlp_ready"], 2 * MC)
                elif v >= 3:
                    pe.wait_ge(S["h_ready"], v - 2)
                for k in range(KC):
                    mm = t_.matmul(fill(4 * MC + v)[:], deT[:, k, e * P:(e + 1) * P], xnT[:, k, half * 512:half * 512 + 512], start=k == 0, stop=k == KC - 1)
                mm.then_inc(S["h_done"], 1)
                if v == 0:
                    y_transposes(NT - 1)

            pe.wait_ge(S["late_in"], 48)
            pe.wait_ge(S["yT_ready"], NT)
            pe.wait_ge(S["mlp_ready"], 2 * MC)

            def prob_transposes(g):
                pe.wait_ge(S["prob_ready"], g + 1)
                if g == 0:
                    pe.wait_ge(S["beyond2_ready"], 1)
                if g >= 2:
                    pe.wait_ge(S["coef_ready"], g - 1)
                for e in range(EC):
                    mm = t_.transpose(bank[3 + g % 2][:, e * P:(e + 1) * P], prob[:, g, 2 * e:2 * e + 2, :].rearrange("p i j -> p (i j)"), ident)
                mm.then_inc(S["pT_done"], 1)

            prob_transposes(0)
            for g in range(NG):
                o = fill(4 * MC + 2 * EC + g)[:, 0:HID]
                if g < 3:
                    pe.wait_ge(S["h_ready"], 2 * EC - 3 + g + 1)
                else:
                    pe.wait_ge(S["fin_ready"], g - 2)
                for m in range(MC):
                    t_.matmul(o, actT[:, m, group_cols(g)], down_sb[:, m, :], start=m == 0, stop=False)
                for hg in range(HG):
                    t_.matmul(o, yT[:, hg, group_cols(g)], wo_sb[:, hg, :], start=False, stop=False)
                if g + 1 < NG:
                    prob_transposes(g + 1)
                pe.wait_ge(S["coef_ready"], g + 1)
                for e in range(EC):
                    mm = t_.matmul(o, coefT[:, e, g % 2, :], ue_sb[:, e, :], start=False, stop=e == EC - 1)
                mm.then_inc(S["fin_done"], 1)

        @block.vector
        def _(dve):
            v = nc.vector
            for T in range(NG // 2):
                dve.wait_ge(S[f"x{T}_in"], 16)
                for g in (2 * T, 2 * T + 1):
                    v.bn_stats(stats[:, g, :], x_sb[:, g, :]).then_inc(S["stat_ready"], 1)
                for g in (2 * T, 2 * T + 1):
                    dve.wait_ge(S["stat_ready"], g + 1)
                    v.bn_aggr(mv[:, g, :], stats[:, g, :]).then_inc(S["aggr_ready"], 1)
                dve.wait_ge(S["aggr_ready"], 2 * T + 2)
                v.tensor_scalar(std[:, 2 * T:2 * T + 2], mv[:, 2 * T:2 * T + 2, 1], EPS_LN, None, ALU.add).then_inc(S["std_in"], 1)
            for T in range(NG // 2):
                dve.wait_ge(S["std_ready"], T + 1)
                v.reciprocal(rstd[:, 2 * T:2 * T + 2], std[:, 2 * T:2 * T + 2]).then_inc(S["rstd_ready"], 1)
                dve.wait_ge(S["rstd_ready"], T + 1)
                for g in (2 * T, 2 * T + 1):
                    if g >= 2:
                        dve.wait_ge(S["xnT_done"], g - 1)
                    v.tensor_scalar(xn[:, g % 2, :], x_sb[:, g, :], mv[:, g, 0:1], rstd[:, g:g + 1], ALU.subtract, ALU.mult).then_inc(S["xn_ready"], 1)
            dve.wait_ge(S["consts_in"], 16)
            v.tensor_copy(keyno[:].rearrange("p j b -> p (j b)"), con("keyno")).then_inc(S["bf_consts"], 1)
            v.tensor_copy(rankweight[:], con("rankweight")).then_inc(S["bf_consts"], 1)
            for half in range(2):
                dve.wait_ge(S["qr_done"], half + 1)
                v.tensor_copy(qrT[:, half * 512:half * 512 + 512], bank[2 + half][:]).then_inc(S["qrT_ready"], 1)
            dve.wait_ge(S["z_done"], 1)
            dve.wait_ge(S["bias_in"], 32)
            v.tensor_tensor(zb[:], bank[6][:, 0:NT * HEADS].rearrange("p (t h) -> p t h", h=HEADS), bg_sb[:].unsqueeze(1).broadcast_to([P, NT, HEADS]), ALU.add).then_inc(S["zb_ready"], 1)

            def top8(g):
                T, j = divmod(g, 2)
                for side in range(2):
                    if g == 0:
                        dve.wait_ge(S["route_ready"], side + 1)
                    v.max(top[:, side, g, :], route[:, side, g, :]).then_inc(S["top_ready"], 1)
                for side in range(2):
                    dve.wait_ge(S["top_ready"], 2 * g + side + 1)
                    v.max_index(topi[:, side, g, :], top[:, side, g, :], route[:, side, g, :]).then_inc(S["topi_ready"], 1)

            def rope(t):
                dve.wait_ge(S["qk_done"], t + 1)
                if t >= 2:
                    dve.wait_ge(S["rot_ready"], 2 * t - 2)
                b = bank[t % 2][:].rearrange("p (h d) -> p h d", d=D)
                for z, w in ((ropeA, "cos"), (ropeB, "sin")):
                    v.tensor_tensor(z[:, t % 2].rearrange("p (h d) -> p h d", d=D), b,
                                    con(w)[:, t * D:(t + 1) * D].unsqueeze(1).broadcast_to([P, 2 * HEADS, D]), ALU.mult).then_inc(S["ropeAB_ready"], 1)

            def feature(t):
                dve.wait_ge(S["relu_ready"], t + 1)
                dve.wait_ge(S["ex_ready"], t + 1)
                v.scalar_tensor_tensor(phi[:, t, :], ex[:, t % 2], 1.0, relu[:, t % 2], ALU.min, ALU.add).then_inc(S["phi_ready"], 1)

            for t in range(NT):
                rope(t)
                if t == 0:
                    dve.wait_ge(S["zexp_ready"], 1)
                    v.tensor_scalar(beta[:], zb[:].rearrange("p t h -> p (t h)"), 1.0, None, ALU.add).then_inc(S["zden_ready"], 1)
                    dve.wait_ge(S["zden_ready"], 1)
                    v.reciprocal(beta[:], beta[:]).then_inc(S["zrec_ready"], 1)
                    dve.wait_ge(S["zrec_ready"], 1)
                    v.tensor_scalar(beta[:], beta[:], BETA_MIN, BETA_MAX, ALU.max, ALU.min).then_inc(S["beta_ready"], 1)
                if t == 2:
                    dve.wait_ge(S["betaT_done"], 1)
                    v.tensor_copy(betaT[:], bank[7][:, 0:P]).then_inc(S["betaT_ready"], 1)
                    dve.wait_ge(S["betaT_ready"], 1)
                    dve.wait_ge(S["ones_ready"], 1)
                    v.tensor_tensor_scan(decT[:], betaT[:], ones[:], 1.0, ALU.mult, ALU.mult).then_inc(S["decT_ready"], 1)
                    dve.wait_ge(S["decT_ready"], 1)
                    v.reciprocal(rdecT[:], decT[:]).then_inc(S["rdecT_ready"], 1)
                    v.tensor_scalar(endcol[:], con("chunkcol"), decT[:, P - 1:P], None, ALU.mult).then_inc(S["endcol_ready"], 1)
                if t == 4:
                    dve.wait_ge(S["rdec_done"], 1)
                    v.tensor_copy(rdec[:].rearrange("p t h -> p (t h)"), bank[7][:, P:2 * P]).then_inc(S["rdec_ready"], 1)
                    dve.wait_ge(S["enddec_done"], 1)
                    v.tensor_copy(enddec[:].rearrange("p k t -> p (k t)"), bank[6][:, 0:HG * NT]).then_inc(S["enddec_ready"], 1)
                top8(t)
                if t >= 1:
                    feature(t - 1)
            feature(NT - 1)

            def choose_pairs():
                dve.wait_ge(S["pair_ready"], 1)
                for g in range(NG):
                    v.max(pair8[:, g, :], pair[:, g, :]).then_inc(S["pair8_ready"], 1)
                for g in range(NG):
                    dve.wait_ge(S["pair8_ready"], g + 1)
                    v.match_replace(marked[:, g, :], pair8[:, g, :], pair[:, g, :], MARK).then_inc(S["marked_ready"], 1)
                dve.wait_ge(S["topi_ready"], 2 * NG)
                v.tensor_copy(xi[:], topi[:, 0]).then_inc(S["xi_ready"], 1)
                v.tensor_copy(yi[:], topi[:, 1]).then_inc(S["xi_ready"], 1)
                dve.wait_ge(S["marked_ready"], NG)
                v.tensor_tensor(chosen[:], pair[:], marked[:], ALU.not_equal).then_inc(S["chosen_ready"], 1)
                dve.wait_ge(S["xi_ready"], 1)
                v.tensor_tensor(xmatch[:], xi[:].unsqueeze(2).broadcast_to([P, NG, NXI, TOPK]),
                                con("xno").rearrange("p (i a) -> p i a", a=TOPK).unsqueeze(1).broadcast_to([P, NG, NXI, TOPK]), ALU.is_equal).then_inc(S["xmatch_ready"], 1)
                dve.wait_ge(S["chosen_ready"], 1)
                v.tensor_reduce(rowcount[:], chosen[:].rearrange("p g (a b) -> p g a b", b=TOPK), AX.X, ALU.add).then_inc(S["rowcount_ready"], 1)

            def rank_y():
                dve.wait_ge(S["bf_consts"], 2)
                dve.wait_ge(S["xi_ready"], 2)
                v.tensor_tensor(ymatch, yi[:].unsqueeze(2).broadcast_to([P, NG, NKEY, TOPK]),
                                keyno[:].unsqueeze(1).broadcast_to([P, NG, NKEY, TOPK]), ALU.is_equal).then_inc(S["ymatch_ready"], 1)
                dve.wait_ge(S["ymatch_ready"], 1)
                ym = ymatch.rearrange("p g j b -> p (g j) b")
                v.tensor_tensor(ym, ym, rankweight[:].unsqueeze(1).broadcast_to([P, NG * NKEY, TOPK]), ALU.mult).then_inc(S["yrank_steps"], 1)
                dve.wait_ge(S["yrank_steps"], 1)
                y4 = yt4.rearrange("p g j b -> p (g j) b")
                v.tensor_tensor(y4, ym[:, :, 0:4], ym[:, :, 4:8], ALU.add).then_inc(S["yrank_steps"], 1)
                dve.wait_ge(S["yrank_steps"], 2)
                v.tensor_tensor(ym[:, :, 0:2], y4[:, :, 0:2], y4[:, :, 2:4], ALU.add).then_inc(S["yrank_steps"], 1)
                dve.wait_ge(S["yrank_steps"], 3)
                v.tensor_tensor(yrank[:].rearrange("p g j -> p (g j)"), ym[:, :, 0], ym[:, :, 1], ALU.add).then_inc(S["yrank_steps"], 1)

            def sums():
                dve.wait_ge(S["psel_ready"], 1)
                v.tensor_reduce(rowsum[:], pexp[:].rearrange("p g (a b) -> p g a b", b=TOPK), AX.X, ALU.add).then_inc(S["rowsum_ready"], 1)
                dve.wait_ge(S["rowsum_ready"], 1)
                v.tensor_reduce(total[:], rowsum[:], AX.X, ALU.add).then_inc(S["total_ready"], 1)
                v.scalar_tensor_tensor(beyond[:], xi[:], float(NXI), rowsum[:], ALU.is_ge, ALU.mult).then_inc(S["beyond_ready"], 1)
                dve.wait_ge(S["total_ready"], 1)
                v.reciprocal(rtotal[:], total[:]).then_inc(S["rtotal_ready"], 1)
                dve.wait_ge(S["beyond_ready"], 1)
                v.tensor_reduce(beyond1[:], beyond[:], AX.X, ALU.add).then_inc(S["beyond1_ready"], 1)
                dve.wait_ge(S["xmatchc_ready"], 1)
                v.tensor_reduce(xcount[:], xmatch[:], AX.X, ALU.add).then_inc(S["xcount_ready"], 1)
                dve.wait_ge(S["xcount_ready"], 1)
                v.tensor_scalar(xlimit[:], xcount[:], -1.0, float(TOPK), ALU.mult, ALU.add).then_inc(S["xlimit_ready"], 1)
                dve.wait_ge(S["rtotal_ready"], 1)
                dve.wait_ge(S["beyond1_ready"], 1)
                v.tensor_tensor(beyond1[:], beyond1[:], rtotal[:], ALU.mult).then_inc(S["beyond1_ready"], 1)

            def prob_mask(g):
                if g == 0:
                    dve.wait_ge(S["xlimit_ready"], 1)
                    dve.wait_ge(S["yrank_steps"], 4)
                v.tensor_tensor(prob[:, g], yrank[:, g].unsqueeze(1).broadcast_to([P, NXI, NKEY]),
                                xlimit[:, g].unsqueeze(2).broadcast_to([P, NXI, NKEY]), ALU.is_gt).then_inc(S["prob0_ready"], 1)

            def mlp(u):
                m, half = divmod(u, 2)
                dve.wait_ge(S["silu_ready"], u + 1)
                dve.wait_ge(S["up_done"], u + 1)
                v.tensor_tensor(actT[:, m, half * 512:half * 512 + 512], sil[:, u % 2], fill(2 * u + 1)[:], ALU.mult).then_inc(S["mlp_ready"], 1)

            def mask(c, first):
                if first == 0 and c >= 1:
                    dve.wait_ge(S["y_done"], c)
                for j in (first, first + 1):
                    dve.wait_ge(S["s_done"], 4 * c + j + 1)
                    v.tensor_tensor(sc[:, j], bank[3 + j % 2][:].rearrange("p (r n) -> p r n", n=P),
                                    con("causal").unsqueeze(1).broadcast_to([P, 4, P]), ALU.mult).then_inc(S["sc_ready"], 1)

            def chunk_sum(c):
                dve.wait_ge(S["u_done"], c + 1)
                if c == 0:
                    dve.wait_ge(S["enddec_ready"], 1)
                else:
                    dve.wait_ge(S["state_ready"], 2 * c)
                for hg in range(HG):
                    v.scalar_tensor_tensor(upd[:, hg], bank[7][:, hg * HPG * E1:(hg + 1) * HPG * E1], enddec[:, hg, c:c + 1],
                                           con("headblock"), ALU.mult, ALU.mult).then_inc(S["upd_ready"], 1)

            def advance_state(c):
                for hg in range(HG):
                    dve.wait_ge(S["upd_ready"], 2 * c + hg + 1)
                    if c == 0:
                        v.tensor_copy(state[:, hg], upd[:, hg]).then_inc(S["state_ready"], 1)
                    else:
                        v.scalar_tensor_tensor(state[:, hg], state[:, hg], enddec[:, hg, c:c + 1], upd[:, hg], ALU.mult, ALU.add).then_inc(S["state_ready"], 1)

            def normalise(c):
                yb = bank[6][:, 0:HEADS * E1].rearrange("p (h e) -> p h e", e=E1)
                dve.wait_ge(S["y_done"], c + 1)
                v.scalar_tensor_tensor(den[:], rdec[:, c, :], EPS_DEN, yb[:, :, D], ALU.mult, ALU.add).then_inc(S["den_ready"], 1)
                dve.wait_ge(S["den_ready"], c + 1)
                v.reciprocal(rden[:], den[:]).then_inc(S["rden_ready"], 1)
                dve.wait_ge(S["rden_ready"], c + 1)
                if c >= 1:
                    dve.wait_ge(S["yT_done"], c)
                v.tensor_tensor(y[:], yb[:, :, 0:D], rden[:].unsqueeze(2).broadcast_to([P, HEADS, D]), ALU.mult).then_inc(S["y_ready"], 1)

            def finish(g):
                nc.vector.wait_ge(S["fin_done"], g + 1)
                if g == 0:
                    nc.vector.wait_ge(S["xb_ready"], 1)
                nc.vector.tensor_tensor(fin[:, g], fill(4 * MC + 2 * EC + g)[:, 0:HID], x_sb[:, g], ALU.add).then_inc(S["fin_ready"], 1)

            for c in range(NT):
                mlp(2 * c)
                mask(c, 0)
                mask(c, 2)
                if c < NT - 1:
                    chunk_sum(c)
                mlp(2 * c + 1)
                normalise(c)
                if c < NT - 1:
                    advance_state(c)
                if c == 0:
                    choose_pairs()
                if c == 1:
                    rank_y()
                if c == 2:
                    sums()
                if c == 3:
                    for g in range(4):
                        prob_mask(g)
                if c == 4:
                    for g in range(4, NG):
                        prob_mask(g)
            dve.wait_ge(S["prob_ready"], NG)
            dve.wait_ge(S["beyond1_ready"], 2)
            v.tensor_tensor(prob[:, :, NXI - 1, NKEY - 1], prob[:, :, NXI - 1, NKEY - 1], beyond1[:], ALU.add).then_inc(S["beyond2_ready"], 1)
            for g in range(NG):
                dve.wait_ge(S["pT_done"], g + 1)
                if g == 0:
                    dve.wait_ge(S["h_ready"], 2 * EC)
                if g >= 2:
                    dve.wait_ge(S["fin_done"], g - 1)
                v.tensor_tensor(coefT[:, :, g % 2, :], bank[3 + g % 2][:].rearrange("p (e n) -> p e n", n=P), hT[:, :, group_cols(g)], ALU.mult).then_inc(S["coef_ready"], 1)
                if g >= 1:
                    finish(g - 1)
            finish(NG - 1)


def constants():
    import numpy as np
    cols, n = const_columns()
    c = np.zeros((P, n), np.float32)

    def put(name, a):
        lo, hi = cols[name]
        c[:, lo:hi] = np.broadcast_to(np.asarray(a, np.float32).reshape(-1 if np.ndim(a) == 1 else P, *([] if np.ndim(a) == 1 else [-1])), (P, hi - lo))

    p = np.arange(P)
    put("ident", np.eye(P))
    put("causal", p[:, None] <= p[None, :])
    put("headblock", np.repeat(p[:, None] // D == np.arange(HPG)[None], E1, axis=1))
    half = D // 2
    inv_freq = np.float32(1.0) / np.float32(10000.0) ** (np.arange(half, dtype=np.float32) / np.float32(half))
    token = (np.arange(NT)[None, :] * P + p[:, None]).astype(np.float32) % np.float32(N_TOK)
    freqs = token[:, :, None] * inv_freq.astype(np.float32)
    put("cos", np.concatenate([np.cos(freqs)] * 2, axis=2).reshape(P, -1))
    put("sin", np.concatenate([np.sin(freqs), -np.sin(freqs)], axis=2).reshape(P, -1))
    put("parity", (p[:, None] // D) % 2 == np.arange(2)[None])
    put("keyno", np.repeat(np.arange(NKEY), TOPK))
    put("rankweight", TOPK - np.arange(TOPK))
    put("xno", np.repeat(np.arange(NXI), TOPK))
    put("chunkcol", p[:, None] // HEADS == np.arange(NT)[None])
    put("headrows", (p[:, None] % HEADS == (np.arange(HEADS).repeat(D))[None]))
    return c


_INS = ["L0_attn_x", "L0_attn_Wq", "L0_attn_Wk", "L0_attn_Wv", "L0_attn_Wg", "L0_attn_bg", "L0_attn_Wo", "L0_attn_bo",
        "L0_ffn_W_q", "L0_ffn_keys", "L0_ffn_down_embed", "L0_ffn_up_embed", "L0_ffn_gate_w", "L0_ffn_up_w", "L0_ffn_down_w"]


def kernel(**inputs):
    import numpy as np
    import concourse.bacc as bacc
    from concourse.bass_utils import run_bass_kernel_spmd

    nc = bacc.Bacc("TRN2", target_bir_lowering=False, num_devices=1)
    arrays, args = {}, []
    for name in _INS:
        a = np.ascontiguousarray(inputs[name])
        arrays[name] = a
        args.append(nc.dram_tensor(name, a.shape, mybir.dt.from_np(a.dtype), kind="ExternalInput").ap())
    arrays["constants"] = constants()
    args.append(nc.dram_tensor("constants", arrays["constants"].shape, F32, kind="ExternalInput").ap())
    out = nc.dram_tensor("out", (1, N_TOK, HID), F32, kind="ExternalOutput").ap()
    build(nc, *args, out)
    r = run_bass_kernel_spmd(nc, [arrays], core_ids=[0])
    return r.results[0]["out"]
```

```python
from contextlib import ExitStack

import concourse.bass as bass
from concourse import mybir

F32 = mybir.dt.float32
F32R = mybir.dt.float32r
BF16 = mybir.dt.bfloat16
U32 = mybir.dt.uint32
ALU = mybir.AluOpType
ACT = mybir.ActivationFunctionType
AX = mybir.AxisListType

P = 128
N_TOK = 1024
HID = 256
KC = HID // P
NT = N_TOK // P
NG = NT
HEADS = 16
D = HID // HEADS
E1 = D + 1
HG = 2
HPG = HEADS // HG
INTER = 1024
MC = INTER // P
NEXP = 512
EC = NEXP // P
NKEY = 64
TOPK = 8
NXI = NEXP // NKEY
EPS_DEN = 1e-6
EPS_LN = 1e-5
BETA_MIN, BETA_MAX = 0.8, 0.9995
MARK = -3.0e38
HALVES = 2
HT = N_TOK // HALVES
GPH = NG // HALVES
CPH = NT // HALVES
RANKED = 2
PIECES = 2 * MC + EC

HI, LO = 0, 1
PASSES = ((HI, HI), (HI, LO), (LO, HI))

CONST_PARTS = [("rankweight", TOPK), ("xno", NXI * TOPK), ("chunkcol", NT), ("ident", P), ("cos", NT * D), ("sin", NT * D),
               ("headrows", HG * P), ("causal", P), ("headblock", HPG * E1), ("keyno", NKEY * TOPK)]


def const_columns():
    at, out = 0, {}
    for name, n in CONST_PARTS:
        out[name] = (at, at + n)
        at += n
    return out, at


def build(nc, x, Wq, Wk, Wv, Wg, bg, Wo, bo, W_qr, keys, down_embed, up_embed, gate_w, up_w, down_w, consts, out):
    cols, n_const = const_columns()
    n_kept, n_rope, n_brief = cols["ident"][0], cols["headrows"][0], n_const - cols["headrows"][0]
    x_g = x.rearrange("a (t p j) d -> p (a t) (j d)", p=P, j=2)
    out_g = out.rearrange("a (t p j) d -> p (a t) (j d)", p=P, j=2)

    def rows(w):
        return w.rearrange("(k p) n -> p k n", p=P)

    with ExitStack() as ctx:
        def sb(name, shape, dt=F32):
            return ctx.enter_context(nc.sbuf_tensor(name, shape, dt))

        def sem(name):
            return ctx.enter_context(nc.semaphore(name))

        bank = [ctx.enter_context(nc.psum_tensor(f"bank{i}", [P, 512], F32)) for i in range(8)]

        xnT = sb("xnT", [P, 2, KC, N_TOK], F32R)
        gate_p = sb("gate_p", [P, 2, KC, INTER], F32R)
        up_p = sb("up_p", [P, 2, KC, INTER], F32R)
        down_p = sb("down_p", [P, 2, MC, HID], F32R)
        ue_p = sb("ue_p", [P, 2, EC, HID], F32R)
        deT = sb("deT", [P, 2, KC, NEXP], F32R)
        wo_p = sb("wo_p", [P, 2, KC, HID], F32R)
        yT = sb("yT", [P, 2, HG, HT], F32R)
        act_p = sb("act_p", [P, 2, MC, HT], F32R)
        early_p = act_p[:, :, :, :].rearrange("p s m n -> p s (m n)")
        ring = sb("ring", [P, 2048], F32R)
        qrT = ring[:, :].rearrange("p (s n) -> p s n", s=2)
        qk4 = ring[:, :].rearrange("p (r w i n) -> p r w i n", r=4, w=2, i=2)
        coef = ring[:, :].rearrange("p (b s e n) -> p b s e n", b=2, s=2, e=EC)
        qk_tok = sb("qk_tok", [P, 2, HEADS, 4, D], F32R)
        identr = sb("identr", [P, P], F32R)

        cst = sb("cst", [P, n_kept])
        causal = sb("causal", [P, P], BF16)
        headblock = sb("headblock", [P, HPG * E1], BF16)
        work = sb("work", [P, 2048])
        x_sb = work[:, :].rearrange("p (g n) -> p g n", g=NG)
        ROPES = 3
        ropeA = work[:, 512:2048].rearrange("p (b n) -> p b n", b=ROPES)
        pair = work[:, 0:512].rearrange("p (g n) -> p g n", g=NG)
        ymatch = work[:, 1024:1536].bitcast(BF16).rearrange("p (g j b) -> p g j b", g=RANKED, b=TOPK)
        xmatch = work[:, 1792:2048].bitcast(BF16).rearrange("p (g i a) -> p g i a", g=NG, a=TOPK)
        yt4 = work[:, 1536:1792].bitcast(BF16).rearrange("p (g j b) -> p g j b", g=RANKED, b=4)
        hT = work[:, :].rearrange("p (e n) -> p e n", e=EC)
        N_EARLY = KC * 2 * HID + KC * (HID + HEADS) + KC * P + 2 * 2 * NKEY
        early = sb("early", [P, N_EARLY])
        sc = early[:, 0:2048].rearrange("p (u s i n) -> p u s i n", u=2, s=2, i=4)

        WVG, WQR, KEYS, WQK = range(4)
        EARLY = ((KC, HID + HEADS), (KC, P), (2, 2 * NKEY), (KC, 2 * HID))

        def early_at(i):
            return sum(k * n for k, n in EARLY[:i])

        def early_w(i, part=None):
            k, n = EARLY[i]
            t = early if part is None else early_p[:, part]
            return t[:, early_at(i):early_at(i + 1)].rearrange("p (k n) -> p k n", k=k)

        prob = sb("prob", [P, GPH, NXI, NKEY])
        stage = prob[:, :, :, :].rearrange("p g i j -> p (g i j)").rearrange("p (s n) -> p s n", s=2)
        de_sb = sb("de_sb", [P, EC, HID])
        sil = de_sb[:, :, :].rearrange("p (u e) n -> p u (e n)", u=2)
        phi = sb("phi", [P, NT, 2 * HID])
        fin = phi[:, 0:NG // 2, :].rearrange("p t (j n) -> p (t j) n", j=2)
        v1 = sb("v1", [P, NT, HEADS, E1])
        xn = sb("xn", [P, 2, HID])
        chosen = xn[:, :, :].rearrange("p a n -> p (a n)").rearrange("p (g n) -> p g n", g=NG)
        qT = xn[:, 0, :].rearrange("p (k n) -> p k n", k=HG)
        y = xn[:, 1, :].rearrange("p (h d) -> p h d", d=D)
        stats = sb("stats", [P, NG, 6])
        mv = sb("mv", [P, NG, 2])
        std = sb("std", [P, NG])
        rstd = sb("rstd", [P, NG])
        bg_sb = sb("bg_sb", [P, HEADS])
        route = sb("route", [P, 2, NG, NKEY])
        tops = sb("tops", [P, HID])
        top = tops[:, 0:128].rearrange("p (s g n) -> p s g n", s=2, n=TOPK)
        topi = tops[:, 128:256].bitcast(U32).rearrange("p (s g n) -> p s g n", s=2, n=TOPK)
        bo_sb = tops[:, :]
        xi = sb("xi", [P, NG, TOPK])
        yi = sb("yi", [P, NG, TOPK], BF16)
        rowcount = sb("rowcount", [P, NG, TOPK])
        pair8 = sb("pair8", [P, NG, TOPK])
        rowsum = beyond = pair8
        total = sb("total", [P, NG])
        rtotal = sb("rtotal", [P, NG])
        xcount = sb("xcount", [P, NG, NXI])
        beyond1 = sb("beyond1", [P, NG])
        xw = sb("xw", [P, NG, NXI])
        yw = route[:, 1]
        upd = route[:, 0].rearrange("p g n -> p (g n)")[:, 0:HG * HPG * E1].rearrange("p (k n) -> p k n", k=HG)
        keyno = sb("keyno", [P, NKEY, TOPK], BF16)
        rankweight = sb("rankweight", [P, TOPK], BF16)
        yrank = sb("yrank", [P, NG, NKEY])
        beta, betaT, decT = (yrank[:, 2 * i:2 * i + 2, :].rearrange("p g n -> p (g n)") for i in range(3))
        recur = sb("recur", [P, HG * HPG * E1])
        state = recur[:, :].rearrange("p (k n) -> p k n", k=HG)
        brief = phi[:, NT - 3:NT, :].rearrange("p t n -> p (t n)")[:, 0:n_brief]

        def con(name):
            a, b = cols[name]
            if b <= n_kept:
                return cst[:, a:b]
            if name == "ident":
                return yrank[:, 6:8, :].rearrange("p g n -> p (g n)")
            return recur[:, a - cols["cos"][0]:b - cols["cos"][0]] if b <= n_rope else brief[:, a - n_rope:b - n_rope]

        rdec = sb("rdec", [P, NT, HEADS])
        endcol = sb("endcol", [P, NT])
        enddec = sb("enddec", [P, HG, NT])
        den = sb("den", [P, HEADS])
        rden = sb("rden", [P, HEADS])

        ident = identr[:].bitcast(F32)

        START = (3, 2)

        def steps(H, q):
            return [(H * CPH + cl, q - START[H] - 4 * cl) for cl in range(CPH)]

        names = """x0_in x1_in x2_in x3_in consts_in ident_in route_in vg_in qk_in stage0_in stage1_in embed_in bg_in bo_in x_again0 x_again1 x_again2 x_again3
            keys_zero v1_ones identr_ready stat_ready aggr_ready std_in std_ready rstd_ready xn_ready
            xnT_done xnT_hi xnT_lo route_w_hi route_w_lo early_hi v_w_lo qk_w_lo stage_hi stage0_lo stage1_lo qr_done qrT_hi qrT_lo route_done route_ready
            z_ready zb_ready zexp_ready zden_ready zrec_ready beta_ready betaT_done betaT_ready decT_ready rdecT_ready
            rdec_done rdec_ready endcol_ready enddec_done enddec_ready
            qk_done v_done v_ready ropeAB_ready rot_ready feat_in phi_ready kp_ready deT_done deT_hi deT_lo
            top_ready topi_ready xi_ready pair_ready pair8_ready marked_ready chosen_ready pdif_ready pexp_ready
            wdif_ready xw_exp yw_exp psel_ready rowcount_ready rowsum_ready total_ready rtotal_ready
            bf_consts ymatch_ready yrank_steps xmatch_ready xmatchc_ready xcount_ready xlimit_ready beyond_ready beyond1_ready
            xw_ready prob0_ready prob1_ready prob_ready beyond2_ready
            tok_hi tok_lo t_done t_ready_act t_ready_dve qT_done qT_ready s_done sc_ready u_done upd_ready state_ready
            y_done den_ready rden_ready y_ready yT_done yT_hi yT_lo
            gate_done up_done silu_ready mlp_ready act_hi act_lo h_done h_ready pT_done coefprod_ready coef_hi coef_lo
            fin_done xb_ready fin_ready out_done""".split()
        S = {n: sem(n) for n in names}

        block = ctx.enter_context(nc.Block())

        def group_cols(g, within=N_TOK):
            T, j = divmod(g % (2 * within // (2 * P)), 2)
            return slice(T * 2 * P + j, (T + 1) * 2 * P - 1 + j, 2)

        PLACES = PIECES + GPH

        def gate_place(u):
            return (u // MC) * PLACES + 2 * (u % MC)

        def h_place(v):
            return (v // EC) * PLACES + 2 * MC + v % EC

        def fin_place(g):
            return (g // GPH) * PLACES + PIECES + g % GPH

        def place_bank(n):
            return bank[n % 3]

        def wait_place_free(eng, n):
            if n < 3:
                return
            H, q = divmod(n - 3, PLACES)
            if q < 2 * MC and q % 2 == 0:
                eng.wait_ge(S["silu_ready"], H * MC + q // 2 + 1)
            elif q < 2 * MC:
                eng.wait_ge(S["mlp_ready"], H * MC + q // 2 + 1)
            elif q < PIECES:
                eng.wait_ge(S["h_ready"], H * EC + q - 2 * MC + 1)
            else:
                eng.wait_ge(S["fin_ready"], H * GPH + q - PIECES + 1)

        def stage_items():
            for w, dst in ((gate_w, gate_p), (up_w, up_p)):
                for k in range(KC):
                    yield w[k * P:(k + 1) * P, :], INTER, dst[:, :, k, :]
            for i in range(2):
                yield rows(down_w)[:, 4 * i:4 * i + 4, :], 1024, down_p[:, :, 4 * i:4 * i + 4, :].rearrange("p s m n -> p s (m n)")
            yield rows(up_embed), 1024, ue_p[:, :, :, :].rearrange("p s m n -> p s (m n)")
            yield rows(Wo), 512, wo_p[:, :, :, :].rearrange("p s m n -> p s (m n)")

        staged = list(stage_items())

        def wait_split(eng, w):
            eng.wait_ge(S[f"stage{w % 2}_lo"], w // 2 + 1)

        def split_weights(eng, ops, w):
            _src, n, dst = staged[w]
            eng.wait_ge(S["stage_hi"], w + 1)
            ops.tensor_tensor(dst[:, LO], stage[:, w % 2, 0:n], dst[:, HI].bitcast(F32), ALU.subtract).then_inc(S[f"stage{w % 2}_lo"], 1)

        @block.sync
        def _(sp):
            for T in range(NG // 2):
                sp.dma_start(x_sb[:, 2 * T:2 * T + 2, :].rearrange("p j d -> p (j d)"), x_g[:, T, :]).then_inc(S[f"x{T}_in"], 16)
            sp.dma_start(early_w(WQR), rows(W_qr)).then_inc(S["route_in"], 16)
            sp.wait_ge(S["keys_zero"], 1)
            for half in range(2):
                for j in range(2):
                    sp.dma_start(early_w(KEYS)[64 * j:64 * j + 64, half, NKEY * j:NKEY * j + NKEY], keys[half]).then_inc(S["route_in"], 16)
            sp.dma_start(early_w(WVG)[:, :, 0:HID], rows(Wv)).then_inc(S["vg_in"], 16)
            sp.dma_start(early_w(WVG)[:, :, HID:HID + HEADS], rows(Wg)).then_inc(S["vg_in"], 16)
            sp.dma_start(early_w(WQK)[:, :, 0:HID], rows(Wq)).then_inc(S["qk_in"], 16)
            sp.dma_start(early_w(WQK)[:, :, HID:2 * HID], rows(Wk)).then_inc(S["qk_in"], 16)
            for w, (src, n, _dst) in enumerate(staged):
                if w == 1:
                    sp.dma_start(de_sb[:], rows(down_embed)).then_inc(S["embed_in"], 16)
                if w >= 2:
                    wait_split(sp, w - 2)
                dst = stage[:, w % 2, 0:n]
                if w >= 4:
                    dst = dst.rearrange("p (m n) -> p m n", n=HID)
                sp.dma_start(dst, src).then_inc(S[f"stage{w % 2}_in"], 16)
            sp.wait_ge(S["xi_ready"], 2)
            sp.wait_ge(S["wdif_ready"], 2)
            sp.dma_start(bo_sb, bo.rearrange("(a n) -> a n", a=1).broadcast_to([P, HID])).then_inc(S["bo_in"], 16)
            for T in range(NG // 2):
                if T >= 1:
                    sp.wait_ge(S["qT_done"], T)
                sp.wait_ge(S["u_done"], T + 1)
                sp.wait_ge(S["tok_lo"], 4 * T + 4)
                sp.dma_start(phi[:, T, :], x_g[:, T, :]).then_inc(S[f"x_again{T}"], 16)
            for T in range(NG // 2):
                sp.wait_ge(S["fin_ready"], 2 * T + 2)
                sp.dma_start(out_g[:, T, :], phi[:, T, :]).then_inc(S["out_done"], 16)
            sp.wait_ge(S["out_done"], 16 * (NG // 2))

        def tok_parts(c, unit, which):
            src = phi[:, c, which * HID + unit * P:which * HID + (unit + 1) * P].rearrange("p (h d) -> p h d", d=D)
            dst = qk_tok[:, which, unit * HPG:(unit + 1) * HPG, :, :]
            twice = src.unsqueeze(2).broadcast_to([P, HPG, 2, D])
            if which == 0:
                return twice, dst[:, :, 0:4:2, :], dst[:, :, 1:4:2, :]
            return twice, dst[:, :, 0:2, :], dst[:, :, 2:4, :]

        @block.gpsimd
        def _(pool):
            g = nc.gpsimd
            g.dma_start(cst[:], consts[:, 0:n_kept]).then_inc(S["consts_in"], 16)
            g.dma_start(brief, consts[:, n_rope:n_const]).then_inc(S["consts_in"], 16)
            g.dma_start(recur[:, 0:n_rope - cols["cos"][0]], consts[:, cols["cos"][0]:n_rope]).then_inc(S["consts_in"], 16)
            g.dma_start(bg_sb[:], bg.rearrange("(a n) -> a n", a=1).broadcast_to([P, HEADS])).then_inc(S["bg_in"], 16)
            g.memset(early_w(KEYS), 0.0).then_inc(S["keys_zero"], 1)
            g.memset(v1[:], 1.0).then_inc(S["v1_ones"], 1)

            def rotate(t):
                pool.wait_ge(S["ropeAB_ready"], 2 * t + 2)
                a, b = (z.rearrange("p (h s d) -> p h s d", s=2, d=D // 2) for z in (ropeA[:, t % ROPES], phi[:, t]))
                for s in range(2):
                    g.tensor_tensor(a[:, :, s, :], a[:, :, s, :], b[:, :, 1 - s, :], ALU.add).then_inc(S["rot_ready"], 1)

            def key_scale(t):
                pool.wait_ge(S["phi_ready"], t + 1)
                pool.wait_ge(S["rdec_ready"], 1)
                kk = phi[:, t, HID:2 * HID].rearrange("p (h d) -> p h d", d=D)
                g.tensor_tensor(kk, kk, rdec[:, t].unsqueeze(2).broadcast_to([P, HEADS, D]), ALU.mult).then_inc(S["kp_ready"], 1)

            def tok_lo(c, unit):
                pool.wait_ge(S["tok_hi"], 4 * c + 2 * unit + 2)
                for which in range(2):
                    twice, hi, lo = tok_parts(c, unit, which)
                    g.tensor_tensor(lo, twice, hi.bitcast(F32), ALU.subtract).then_inc(S["tok_lo"], 1)

            def act_lo(u):
                pool.wait_ge(S["act_hi"], u + 1)
                g.tensor_tensor(act_p[:, LO, u % MC, :], sil[:, u % 2], act_p[:, HI, u % MC, :].bitcast(F32), ALU.subtract).then_inc(S["act_lo"], 1)

            def pair_sums():
                for side in range(2):
                    pool.wait_ge(S["top_ready"], NG * side + NG)
                g.tensor_tensor(pair.rearrange("p g (a b) -> p g a b", b=TOPK),
                                top[:, 0].unsqueeze(3).broadcast_to([P, NG, TOPK, TOPK]),
                                top[:, 1].unsqueeze(2).broadcast_to([P, NG, TOPK, TOPK]), ALU.add).then_inc(S["pair_ready"], 1)

            def weight_exponents():
                pool.wait_ge(S["topi_ready"], 2 * NG)
                g.tensor_tensor(xw[:], route[:, 0, :, 0:NXI], top[:, 0, :, 0:1].broadcast_to([P, NG, NXI]), ALU.subtract).then_inc(S["wdif_ready"], 1)
                g.tensor_tensor(yw, yw, top[:, 1, :, 0:1].broadcast_to([P, NG, NKEY]), ALU.subtract).then_inc(S["wdif_ready"], 1)

            def pair_exponents():
                pool.wait_ge(S["marked_ready"], NG)
                g.tensor_tensor(pair, pair, pair8[:, :, 0:1].broadcast_to([P, NG, TOPK * TOPK]), ALU.subtract).then_inc(S["pdif_ready"], 1)

            def weigh_pairs():
                pool.wait_ge(S["chosen_ready"], 1)
                pool.wait_ge(S["pexp_ready"], 1)
                g.tensor_tensor(pair, pair, chosen, ALU.mult).then_inc(S["psel_ready"], 1)
                pool.wait_ge(S["xmatch_ready"], 1)
                pool.wait_ge(S["rowcount_ready"], 1)
                g.tensor_tensor(xmatch, xmatch, rowcount[:].unsqueeze(2).broadcast_to([P, NG, NXI, TOPK]), ALU.mult).then_inc(S["xmatchc_ready"], 1)

            def scale_xw():
                pool.wait_ge(S["xw_exp"], 1)
                pool.wait_ge(S["rtotal_ready"], 1)
                g.tensor_tensor(xw[:], xw[:], rtotal[:].unsqueeze(2).broadcast_to([P, NG, NXI]), ALU.mult).then_inc(S["xw_ready"], 1)

            def probabilities(q):
                b = q % GPH
                pool.wait_ge(S["prob0_ready"], q + 1)
                pool.wait_ge(S["yw_exp"], 1)
                g.tensor_tensor(prob[:, b], prob[:, b], yw[:, q].unsqueeze(1).broadcast_to([P, NXI, NKEY]), ALU.mult).then_inc(S["prob1_ready"], 1)
                pool.wait_ge(S["prob1_ready"], q + 1)
                pool.wait_ge(S["xw_ready"], 1)
                g.tensor_tensor(prob[:, b], prob[:, b], xw[:, q].unsqueeze(2).broadcast_to([P, NXI, NKEY]), ALU.mult).then_inc(S["prob_ready"], 1)

            pool.wait_ge(S["early_hi"], 1)
            at_v = slice(early_at(WVG), early_at(WVG + 1))
            g.tensor_tensor(early_p[:, LO, at_v], early[:, at_v], early_p[:, HI, at_v].bitcast(F32), ALU.subtract).then_inc(S["v_w_lo"], 1)
            split_weights(pool, g, 0)
            split_weights(pool, g, 2)
            pair_sums()
            weight_exponents()
            for t in range(NT):
                rotate(t)
                if t == 3:
                    pair_exponents()
                if t == 6:
                    key_scale(0)
            tok_lo(0, 0)
            tok_lo(0, 1)
            act_lo(0)
            key_scale(1)
            for H in range(HALVES):
                for q in range(START[0] if H == 0 else 0, PIECES):
                    if q < 2 * MC and q % 2 == 1:
                        act_lo(H * MC + q // 2)
                    for c, step in steps(H, q):
                        if step == 0 and c + 2 < NT:
                            key_scale(c + 2)
                        if step in (1, 3) and c + 1 < NT:
                            tok_lo(c + 1, step // 2)
                    if H == 0:
                        if q == 5:
                            weigh_pairs()
                        if q == 10:
                            scale_xw()
                        if q in (12, 14, 16, 18):
                            probabilities(q // 2 - 6)
                    elif q in (6, 8, 10, 12):
                        probabilities(q // 2 + 1)
                    if (H, q) in ((0, 15), (0, 19), (1, 1), (1, 3)):
                        T = 2 * H + (q % 15 >= 3)
                        pool.wait_ge(S[f"x_again{T}"], 16)
                        pool.wait_ge(S["bo_in"], 16)
                        g.tensor_tensor(fin[:, 2 * T:2 * T + 2], fin[:, 2 * T:2 * T + 2], bo_sb.unsqueeze(1).broadcast_to([P, 2, HID]), ALU.add).then_inc(S["xb_ready"], 1)

        @block.scalar
        def _(act):
            a = nc.scalar
            a.dma_start(con("ident"), consts[:, cols["ident"][0]:cols["ident"][1]]).then_inc(S["ident_in"], 16)
            def root(T):
                act.wait_ge(S["std_in"], T + 1)
                a.activation(std[:, 2 * T:2 * T + 2], std[:, 2 * T:2 * T + 2], ACT.Sqrt).then_inc(S["std_ready"], 1)

            root(0)
            act.wait_ge(S["ident_in"], 16)
            a.activation(identr[:], con("ident"), ACT.Copy).then_inc(S["identr_ready"], 1)
            root(1)
            root(2)

            def early_hi(i, j, when, count, event):
                act.wait_ge(S[when], count)
                at = slice(early_at(i), early_at(j))
                a.activation(early_p[:, HI, at], early[:, at], ACT.Copy).then_inc(S[event], 1)

            def xnT_hi(g):
                act.wait_ge(S["xnT_done"], g + 1)
                a.activation(xnT[:, HI, :, group_cols(g)], bank[g % 3][:, 0:2 * P].rearrange("p (k n) -> p k n", k=KC), ACT.Copy).then_inc(S["xnT_hi"], 1)

            def qrT_hi(half):
                act.wait_ge(S["qr_done"], half + 1)
                a.activation(qrT[:, HI, half * 512:half * 512 + 512], bank[3 + half][:], ACT.Copy).then_inc(S["qrT_hi"], 1)

            def copy_route(half):
                act.wait_ge(S["route_done"], half + 1)
                a.activation(route[:, half].rearrange("p g n -> p (g n)"), bank[(5, 3)[half]][:], ACT.Copy).then_inc(S["route_ready"], 1)

            def copy_v(t):
                act.wait_ge(S["v_done"], t + 1)
                b = bank[6 + t % 2]
                a.activation(v1[:, t, :, 0:D], b[:, 0:HID].rearrange("p (h d) -> p h d", d=D), ACT.Copy).then_inc(S["v_ready"], 1)
                a.activation(beta[:, t * HEADS:(t + 1) * HEADS], b[:, HID:HID + HEADS], ACT.Copy).then_inc(S["z_ready"], 1)

            def weights_hi(w):
                _src, n, dst = staged[w]
                act.wait_ge(S[f"stage{w % 2}_in"], 16 * (w // 2 + 1))
                a.activation(dst[:, HI], stage[:, w % 2, 0:n], ACT.Copy).then_inc(S["stage_hi"], 1)

            def tok_hi(c, unit):
                act.wait_ge(S["kp_ready"], c + 1)
                if c >= 1:
                    act.wait_ge(S["t_done"], 4 * (c - 1) + 2 * unit + 2)
                for which in range(2):
                    twice, hi, _lo = tok_parts(c, unit, which)
                    a.activation(hi, twice, ACT.Copy).then_inc(S["tok_hi"], 1)

            def silu(u):
                act.wait_ge(S["gate_done"], u + 1)
                if u >= 2:
                    act.wait_ge(S["act_lo"], u - 1)
                a.activation(sil[:, u % 2], place_bank(gate_place(u))[:], ACT.Silu).then_inc(S["silu_ready"], 1)

            def act_hi(u):
                act.wait_ge(S["mlp_ready"], u + 1)
                a.activation(act_p[:, HI, u % MC, :], sil[:, u % 2], ACT.Copy).then_inc(S["act_hi"], 1)

            xnT_hi(0)
            xnT_hi(1)
            root(3)
            early_hi(WQR, WQK, "route_in", 80, "route_w_hi")
            xnT_hi(2)
            xnT_hi(3)
            early_hi(WVG, WQR, "vg_in", 32, "early_hi")
            xnT_hi(4)
            xnT_hi(5)
            early_hi(WQK, WQK + 1, "qk_in", 32, "early_hi")
            xnT_hi(6)
            xnT_hi(7)
            weights_hi(0)
            qrT_hi(0)
            qrT_hi(1)
            weights_hi(1)
            act.wait_ge(S["v1_ones"], 1)
            copy_v(0)
            copy_v(1)
            copy_route(0)
            copy_v(2)
            copy_v(3)
            copy_route(1)
            copy_v(4)
            copy_v(5)
            weights_hi(2)
            copy_v(6)
            copy_v(7)
            for k in range(KC):
                act.wait_ge(S["deT_done"], k + 1)
                a.activation(deT[:, HI, k], bank[(4, 5)[k]][:], ACT.Copy).then_inc(S["deT_hi"], 1)
            act.wait_ge(S["zb_ready"], 1)
            a.activation(beta, beta, ACT.Exp, scale=-1.0).then_inc(S["zexp_ready"], 1)
            weights_hi(3)
            for t in range(NT):
                act.wait_ge(S["rot_ready"], 2 * t + 2)
                a.activation(phi[:, t], ropeA[:, t % ROPES], ACT.Relu).then_inc(S["feat_in"], 1)
                a.activation(ropeA[:, t % ROPES], ropeA[:, t % ROPES], ACT.Exp).then_inc(S["feat_in"], 1)
                if t == 2:
                    act.wait_ge(S["wdif_ready"], 2)
                    a.activation(xw[:], xw[:], ACT.Exp).then_inc(S["xw_exp"], 1)
                    a.activation(yw, yw, ACT.Exp).then_inc(S["yw_exp"], 1)
                if t == 5:
                    act.wait_ge(S["pdif_ready"], 1)
                    a.activation(pair, pair, ACT.Exp).then_inc(S["pexp_ready"], 1)
            tok_hi(0, 0)
            tok_hi(0, 1)
            silu(0)
            silu(1)
            act_hi(0)
            def copy_round(c, r):
                act.wait_ge(S["t_done"], 4 * c + r + 1)
                if c >= 1:
                    act.wait_ge(S["s_done"], 4 * (c - 1) + 2 * (r // 2) + 2)
                if c == CPH and r == 0:
                    act.wait_ge(S["fin_done"], GPH)
                a.activation(qk4[:, r], bank[5][:].rearrange("p (w i n) -> p w i n", w=2, i=2), ACT.Copy).then_inc(S["t_ready_act"], 1)

            def copy_qT(c):
                act.wait_ge(S["qT_done"], c)
                a.activation(qT, bank[7][:, 0:HID].rearrange("p (k n) -> p k n", k=HG), ACT.Copy).then_inc(S["qT_ready"], 1)

            def yT_hi(c):
                act.wait_ge(S["yT_done"], c + 1)
                at = (c % CPH) * P
                a.activation(yT[:, HI, :, at:at + P], bank[7][:, 0:HID].rearrange("p (k n) -> p k n", k=HG), ACT.Copy).then_inc(S["yT_hi"], 1)

            def coef_hi(g):
                act.wait_ge(S["coefprod_ready"], g + 1)
                if g % GPH >= 2:
                    act.wait_ge(S["fin_done"], g - 1)
                a.activation(coef[:, g % 2, HI], hT[:, :, group_cols(g, HT)], ACT.Copy).then_inc(S["coef_hi"], 1)

            def attention(H, q):
                for c, step in steps(H, q):
                    if step == 0:
                        copy_round(c, 0)
                    if step == 2:
                        copy_round(c, 2)
                    if step == 4 and c >= 1:
                        copy_qT(c)
                    if step == 7:
                        yT_hi(c)
                for c, step in steps(H, q):
                    if step in (1, 3) and c + 1 < NT:
                        tok_hi(c + 1, step // 2)

            for H in range(HALVES):
                for q in range(START[0] if H == 0 else 0, PIECES):
                    if q < 2 * MC and q % 2 == 0:
                        silu(H * MC + q // 2)
                    elif q >= 2 * MC:
                        v = H * EC + q - 2 * MC
                        act.wait_ge(S["h_done"], v + 1)
                        if v == 0:
                            act.wait_ge(S["yrank_steps"], 4 * (NG // RANKED))
                        a.activation(hT[:, v % EC, :], place_bank(h_place(v))[:], ACT.Silu).then_inc(S["h_ready"], 1)
                    attention(H, q)
                    if q < 2 * MC and q % 2 == 1:
                        act_hi(H * MC + q // 2)
                    if H == 0 and q in (4, 6, 8, 10):
                        weights_hi(2 + q // 2)
                for i in range(GPH):
                    coef_hi(H * GPH + i)
                    attention(H, PIECES + i)

        @block.tensor
        def _(pe):
            t_ = nc.tensor

            def product(out_, pairs_):
                n = len(pairs_) * len(PASSES)
                i = 0
                for lhs, rhs in pairs_:
                    for a, b in PASSES:
                        mm = t_.matmul(out_, lhs(a), rhs(b), start=i == 0, stop=i == n - 1)
                        i += 1
                return mm

            def gate_or_up(u, w_p, n, event):
                m, half = u % MC, u // MC
                if u == 0:
                    pe.wait_ge(S["xnT_lo"], NG)
                    for w in ((0, 1) if w_p is gate_p else (2, 3)):
                        wait_split(pe, w)
                wait_place_free(pe, n)
                product(place_bank(n)[:], [(lambda s, k=k: w_p[:, s, k, m * P:(m + 1) * P], lambda s, k=k: xnT[:, s, k, half * HT:(half + 1) * HT])
                                           for k in range(KC)]).then_inc(S[event], 1)

            PRELUDE = ((0, gate_p, gate_place(0), "gate_done"), (0, up_p, gate_place(0) + 1, "up_done"), (1, gate_p, gate_place(1), "gate_done"))

            pe.wait_ge(S["identr_ready"], 1)

            def transpose_xn(g):
                pe.wait_ge(S["xn_ready"], g + 1)
                if g >= 3:
                    pe.wait_ge(S["xnT_lo"], g - 2)
                for k in range(KC):
                    mm = t_.transpose(bank[g % 3][:, k * P:(k + 1) * P], xn[:, g % 2, k * P:(k + 1) * P], ident)
                mm.then_inc(S["xnT_done"], 1)

            def queries(half):
                pe.wait_ge(S["route_w_lo"], 1)
                pe.wait_ge(S["xnT_lo"], 4 * half + 4)
                product(bank[3 + half][:], [(lambda s, k=k: early_w(WQR, s)[:, k, :], lambda s, k=k: xnT[:, s, k, half * 512:half * 512 + 512])
                                            for k in range(KC)]).then_inc(S["qr_done"], 1)

            def routing(half):
                pe.wait_ge(S["qrT_lo"], half + 1)
                for i in range(4):
                    c = (4 * half + i) * P
                    mm = product(bank[(5, 3)[half]][:, i * P:(i + 1) * P], [(lambda s: qrT[:, s, c:c + P], lambda s: early_w(KEYS, s)[:, half, :])])
                mm.then_inc(S["route_done"], 1)

            def v_and_z(t):
                if t == 0:
                    pe.wait_ge(S["v_w_lo"], 1)
                if t % 2 == 0:
                    pe.wait_ge(S["xnT_lo"], t + 2)
                if t >= 2:
                    pe.wait_ge(S["z_ready"], t - 1)
                product(bank[6 + t % 2][:, 0:HID + HEADS], [(lambda s, k=k: xnT[:, s, k, t * P:(t + 1) * P], lambda s, k=k: early_w(WVG, s)[:, k, :])
                                                            for k in range(KC)]).then_inc(S["v_done"], 1)

            for g in range(NG):
                transpose_xn(g)
            queries(0)
            queries(1)
            v_and_z(0)
            v_and_z(1)
            routing(0)
            v_and_z(2)
            v_and_z(3)
            routing(1)
            v_and_z(4)
            v_and_z(5)
            v_and_z(6)
            v_and_z(7)
            pe.wait_ge(S["embed_in"], 16)
            pe.wait_ge(S["route_ready"], 2)
            for k in range(KC):
                for e in range(EC):
                    mm = t_.transpose(bank[(4, 5)[k]][:, e * P:(e + 1) * P], de_sb[:, e, k * P:(k + 1) * P], ident)
                mm.then_inc(S["deT_done"], 1)
            pe.wait_ge(S["qk_w_lo"], 1)
            pe.wait_ge(S["z_ready"], NT)
            for t in range(NT):
                if t >= 2:
                    pe.wait_ge(S["ropeAB_ready"], 2 * (t - 1))
                product(bank[6 + t % 2][:], [(lambda s, k=k: xnT[:, s, k, t * P:(t + 1) * P], lambda s, k=k: early_w(WQK, s)[:, k, :])
                                             for k in range(KC)]).then_inc(S["qk_done"], 1)
                if t == 1:
                    pe.wait_ge(S["beta_ready"], 1)
                    pe.wait_ge(S["deT_lo"], KC)
                    t_.transpose(bank[5][:, 0:P], beta, ident).then_inc(S["betaT_done"], 1)
                if t in (2, 4, 6):
                    gate_or_up(*PRELUDE[t // 2 - 1])
                if t == 4:
                    pe.wait_ge(S["rdecT_ready"], 1)
                    t_.transpose(bank[3][:, 0:P], decT, ident).then_inc(S["rdec_done"], 1)
                    pe.wait_ge(S["consts_in"], 48)
                    for hg in range(HG):
                        mm = t_.matmul(bank[4][:, hg * NT:(hg + 1) * NT], con("headrows")[:, hg * P:(hg + 1) * P], endcol[:], start=True, stop=True)
                    mm.then_inc(S["enddec_done"], 1)

            def down_embed_products(v):
                e, half = v % EC, v // EC
                n = h_place(v)
                wait_place_free(pe, n)
                if v == 0:
                    pe.wait_ge(S["deT_lo"], KC)
                product(place_bank(n)[:], [(lambda s, k=k: deT[:, s, k, e * P:(e + 1) * P], lambda s, k=k: xnT[:, s, k, half * HT:(half + 1) * HT])
                                           for k in range(KC)]).then_inc(S["h_done"], 1)

            def transpose_round(c, r):
                pe.wait_ge(S["tok_lo"], 4 * c + 2 * (r // 2) + 2)
                if c == 0 and r == 0:
                    pe.wait_ge(S["betaT_ready"], 1)
                if r % 2 == 1:
                    pe.wait_ge(S["t_ready_act"], 2 * c + r // 2 + 1)
                elif c >= 1 or r >= 2:
                    pe.wait_ge(S["t_ready_dve"], 2 * c + r // 2)
                for which in range(2):
                    for i in range(2):
                        h = 4 * r + 2 * i
                        mm = t_.matmul(bank[5][:, (2 * which + i) * P:(2 * which + i + 1) * P],
                                       qk_tok[:, which, h:h + 2, :, :].rearrange("p h s d -> p (h s d)"), identr[:], start=True, stop=True)
                mm.then_inc(S["t_done"], 1)

            def scores(c, unit):
                pe.wait_ge(S["t_ready_act"], 2 * c + unit + 1)
                pe.wait_ge(S["t_ready_dve"], 2 * c + unit + 1)
                n = 2 * c + unit
                if n >= 1:
                    pe.wait_ge(S["sc_ready"], 2 * n)
                else:
                    pe.wait_ge(S["rdec_ready"], 1)
                    pe.wait_ge(S["enddec_ready"], 1)
                for i in range(4):
                    for odd in range(2):
                        rws = slice(64 * odd, 64 * odd + 64)
                        mm = t_.matmul(bank[3 + odd][:, i * P:(i + 1) * P], qk4[rws, 2 * unit + i // 2, 1, i % 2, :],
                                       qk4[rws, 2 * unit + i // 2, 0, i % 2, :], start=True, stop=True)
                        if i == 3:
                            mm.then_inc(S["s_done"], 1)

            def chunk_update(c):
                if c == 0:
                    pe.wait_ge(S["ropeAB_ready"], 2 * NT)
                elif c >= 2:
                    pe.wait_ge(S["qT_ready"], c - 1)
                    pe.wait_ge(S["yT_lo"], c - 1)
                for hg in range(HG):
                    mm = t_.matmul(bank[7][:, hg * HPG * E1:(hg + 1) * HPG * E1], phi[:, c, HID + hg * P:HID + (hg + 1) * P],
                                   v1[:, c, hg * HPG:(hg + 1) * HPG, :].rearrange("p h e -> p (h e)"), start=True, stop=True)
                mm.then_inc(S["u_done"], 1)

            def q_transposes(c):
                pe.wait_ge(S["yT_lo"], c)
                pe.wait_ge(S["upd_ready"], 2 * min(c + 1, NT - 1))
                if c >= 2:
                    pe.wait_ge(S["y_done"], c)
                for k in range(HG):
                    mm = t_.transpose(bank[7][:, k * P:(k + 1) * P], phi[:, c, k * P:(k + 1) * P], ident)
                mm.then_inc(S["qT_done"], 1)

            def y_transposes(c):
                pe.wait_ge(S["y_ready"], c + 1)
                if c >= 1:
                    pe.wait_ge(S["qT_ready"], c)
                pe.wait_ge(S["upd_ready"], 2 * min(c + 2 if c % CPH < CPH - 1 else c + 1, NT - 1))
                for k in range(HG):
                    mm = t_.transpose(bank[7][:, k * P:(k + 1) * P], y[:, k * HPG:(k + 1) * HPG, :].rearrange("p h d -> p (h d)"), ident)
                mm.then_inc(S["yT_done"], 1)

            def outputs(c):
                first = True
                if c >= 1:
                    pe.wait_ge(S["y_ready"], c)
                    pe.wait_ge(S["state_ready"], 2 * c)
                    pe.wait_ge(S["qT_ready"], c)
                    for hg in range(HG):
                        t_.matmul(bank[6][:, hg * HPG * E1:(hg + 1) * HPG * E1], qT[:, hg, :], state[:, hg, :], start=first, stop=False, skip_group_check=True)
                        first = False
                pe.wait_ge(S["sc_ready"], 4 * c + 4)
                for h in range(HEADS):
                    unit, i, odd = h // HPG, (h % HPG) // 2, h % 2
                    mm = t_.matmul(bank[6][:, h * E1:(h + 1) * E1], sc[:, unit, odd, i, :], v1[:, c, h, :], start=first, stop=h == HEADS - 1, skip_group_check=True)
                    first = False
                mm.then_inc(S["y_done"], 1)

            def prob_transposes(g):
                pe.wait_ge(S["prob_ready"], g + 1)
                pe.wait_ge(S["beyond2_ready"], g // GPH + 1)
                if g % GPH >= 2:
                    pe.wait_ge(S["coefprod_ready"], g - 1)
                elif g % GPH == 0:
                    pe.wait_ge(S["sc_ready"], 4 * CPH * (g // GPH + 1))
                for e in range(EC):
                    mm = t_.transpose(bank[3 + g % 2][:, e * P:(e + 1) * P], prob[:, g % GPH, 2 * e:2 * e + 2, :].rearrange("p i j -> p (i j)"), ident)
                mm.then_inc(S["pT_done"], 1)

            def attention(H, q):
                for c, step in steps(H, q):
                    if step == 4:
                        scores(c, 1)
                        if c >= 1:
                            q_transposes(c)
                    if step == 5:
                        outputs(c)
                    if step == 7:
                        y_transposes(c)
                for c, step in steps(H, q):
                    if step in (0, 1, 3):
                        transpose_round(c, step)
                    if step == 2:
                        scores(c, 0)
                        transpose_round(c, 2)
                        if c < NT - 1:
                            chunk_update(c)

            for H in range(HALVES):
                for q in range(START[0] if H == 0 else 0, PIECES):
                    if q < 2 * MC:
                        u = H * MC + q // 2
                        if q % 2 == 0:
                            gate_or_up(u, gate_p, gate_place(u), "gate_done")
                        else:
                            gate_or_up(u, up_p, gate_place(u) + 1, "up_done")
                    else:
                        down_embed_products(H * EC + q - 2 * MC)
                    attention(H, q)
                prob_transposes(H * GPH)
                for g in range(H * GPH, (H + 1) * GPH):
                    n = fin_place(g)
                    o = place_bank(n)[:, 0:HID]
                    wait_place_free(pe, n)
                    pe.wait_ge(S["act_lo"], (H + 1) * MC)
                    gc = group_cols(g, HT)
                    if g + 1 < (H + 1) * GPH:
                        prob_transposes(g + 1)
                    attention(H, PIECES + g % GPH)
                    if g == 0:
                        for w in (-2, -1):
                            wait_split(pe, len(staged) + w)
                    first = True
                    for m in range(MC):
                        for a, b in PASSES:
                            t_.matmul(o, act_p[:, a, m, gc], down_p[:, b, m, :], start=first, stop=False)
                            first = False
                    pe.wait_ge(S["coef_lo"], g + 1)
                    for e in range(EC):
                        for a, b in PASSES:
                            t_.matmul(o, coef[:, g % 2, a, e, :], ue_p[:, b, e, :], start=False, stop=False)
                    pe.wait_ge(S["yT_lo"], 2 * (g // 2) + 2)
                    for k in range(HG):
                        for a, b in PASSES:
                            mm = t_.matmul(o, yT[:, a, k, gc], wo_p[:, b, k, :], start=False, stop=k == HG - 1 and (a, b) == PASSES[-1])
                    mm.then_inc(S["fin_done"], 1)

        @block.vector
        def _(dve):
            v = nc.vector
            def statistics(T):
                dve.wait_ge(S[f"x{T}_in"], 16)
                for g in (2 * T, 2 * T + 1):
                    v.bn_stats(stats[:, g, :], x_sb[:, g, :]).then_inc(S["stat_ready"], 1)
                for g in (2 * T, 2 * T + 1):
                    dve.wait_ge(S["stat_ready"], g + 1)
                    v.bn_aggr(mv[:, g, :], stats[:, g, :]).then_inc(S["aggr_ready"], 1)
                dve.wait_ge(S["aggr_ready"], 2 * T + 2)
                v.tensor_scalar(std[:, 2 * T:2 * T + 2], mv[:, 2 * T:2 * T + 2, 1], EPS_LN, None, ALU.add).then_inc(S["std_in"], 1)

            def xnT_lo(g):
                dve.wait_ge(S["xnT_hi"], g + 1)
                gc = group_cols(g)
                v.tensor_tensor(xnT[:, LO, :, gc], bank[g % 3][:, 0:2 * P].rearrange("p (k n) -> p k n", k=KC), xnT[:, HI, :, gc].bitcast(F32),
                                ALU.subtract).then_inc(S["xnT_lo"], 1)

            def qrT_lo(half):
                dve.wait_ge(S["qrT_hi"], half + 1)
                v.tensor_tensor(qrT[:, LO, half * 512:half * 512 + 512], bank[3 + half][:], qrT[:, HI, half * 512:half * 512 + 512].bitcast(F32),
                                ALU.subtract).then_inc(S["qrT_lo"], 1)

            statistics(0)
            statistics(1)
            for T in range(NG // 2):
                dve.wait_ge(S["std_ready"], T + 1)
                v.reciprocal(rstd[:, 2 * T:2 * T + 2], std[:, 2 * T:2 * T + 2]).then_inc(S["rstd_ready"], 1)
                dve.wait_ge(S["rstd_ready"], T + 1)
                for g in (2 * T, 2 * T + 1):
                    if g >= 2:
                        dve.wait_ge(S["xnT_done"], g - 1)
                    v.tensor_scalar(xn[:, g % 2, :], x_sb[:, g, :], mv[:, g, 0:1], rstd[:, g:g + 1], ALU.subtract, ALU.mult).then_inc(S["xn_ready"], 1)
                    if g >= 2:
                        xnT_lo(g - 2)
                if T + 2 < NG // 2:
                    statistics(T + 2)
            xnT_lo(NG - 2)
            xnT_lo(NG - 1)
            dve.wait_ge(S["route_w_hi"], 1)
            at = slice(early_at(WQR), early_at(WQK))
            v.tensor_tensor(early_p[:, LO, at], early[:, at], early_p[:, HI, at].bitcast(F32), ALU.subtract).then_inc(S["route_w_lo"], 1)
            dve.wait_ge(S["early_hi"], 2)
            at = slice(early_at(WQK), N_EARLY)
            v.tensor_tensor(early_p[:, LO, at], early[:, at], early_p[:, HI, at].bitcast(F32), ALU.subtract).then_inc(S["qk_w_lo"], 1)
            qrT_lo(0)
            qrT_lo(1)
            dve.wait_ge(S["consts_in"], 48)
            for dst, src in ((keyno[:].rearrange("p j b -> p (j b)"), "keyno"), (rankweight[:], "rankweight"), (causal[:], "causal"), (headblock[:], "headblock")):
                v.tensor_copy(dst, con(src)).then_inc(S["bf_consts"], 1)
            split_weights(dve, v, 1)
            for side in range(2):
                dve.wait_ge(S["route_ready"], side + 1)
                for g in range(NG):
                    v.max(top[:, side, g, :], route[:, side, g, :]).then_inc(S["top_ready"], 1)
                for g in range(NG):
                    dve.wait_ge(S["top_ready"], NG * side + g + 1)
                    v.max_index(topi[:, side, g, :], top[:, side, g, :], route[:, side, g, :]).then_inc(S["topi_ready"], 1)
            dve.wait_ge(S["z_ready"], NT)
            dve.wait_ge(S["bg_in"], 16)
            b3 = beta.rearrange("p (t h) -> p t h", h=HEADS)
            v.tensor_tensor(b3, b3, bg_sb[:].unsqueeze(1).broadcast_to([P, NT, HEADS]), ALU.add).then_inc(S["zb_ready"], 1)
            for k in range(KC):
                dve.wait_ge(S["deT_hi"], k + 1)
                v.tensor_tensor(deT[:, LO, k], bank[(4, 5)[k]][:], deT[:, HI, k].bitcast(F32), ALU.subtract).then_inc(S["deT_lo"], 1)

            def rope(t):
                dve.wait_ge(S["qk_done"], t + 1)
                if t >= ROPES:
                    dve.wait_ge(S["phi_ready"], t - ROPES + 1)
                if t == NT - 3:
                    dve.wait_ge(S["enddec_done"], 1)
                b = bank[6 + t % 2][:].rearrange("p (h d) -> p h d", d=D)
                for z, w in ((ropeA[:, t % ROPES], "cos"), (phi[:, t], "sin")):
                    v.tensor_tensor(z.rearrange("p (h d) -> p h d", d=D), b,
                                    con(w)[:, t * D:(t + 1) * D].unsqueeze(1).broadcast_to([P, 2 * HEADS, D]), ALU.mult).then_inc(S["ropeAB_ready"], 1)

            def feature(t):
                dve.wait_ge(S["feat_in"], 2 * t + 2)
                v.scalar_tensor_tensor(phi[:, t, :], ropeA[:, t % ROPES], 1.0, phi[:, t], ALU.min, ALU.add).then_inc(S["phi_ready"], 1)

            def mlp(u):
                dve.wait_ge(S["silu_ready"], u + 1)
                dve.wait_ge(S["up_done"], u + 1)
                v.tensor_tensor(sil[:, u % 2], sil[:, u % 2], place_bank(gate_place(u) + 1)[:], ALU.mult).then_inc(S["mlp_ready"], 1)

            def choose_pairs():
                dve.wait_ge(S["pair_ready"], 1)
                for g in range(NG):
                    v.max(pair8[:, g, :], pair[:, g, :]).then_inc(S["pair8_ready"], 1)
                for g in range(NG):
                    dve.wait_ge(S["pair8_ready"], g + 1)
                    v.match_replace(chosen[:, g, :], pair8[:, g, :], pair[:, g, :], MARK).then_inc(S["marked_ready"], 1)
                dve.wait_ge(S["topi_ready"], 2 * NG)
                v.tensor_copy(xi[:], topi[:, 0]).then_inc(S["xi_ready"], 1)
                v.tensor_copy(yi[:], topi[:, 1]).then_inc(S["xi_ready"], 1)

            def count_pairs():
                dve.wait_ge(S["marked_ready"], NG)
                v.tensor_scalar(chosen, chosen, MARK, None, ALU.is_equal).then_inc(S["chosen_ready"], 1)
                dve.wait_ge(S["chosen_ready"], 1)
                v.tensor_reduce(rowcount[:], chosen.rearrange("p g (a b) -> p g a b", b=TOPK), AX.X, ALU.add).then_inc(S["rowcount_ready"], 1)

            def match_x():
                dve.wait_ge(S["xi_ready"], 1)
                dve.wait_ge(S["phi_ready"], NT)
                v.tensor_tensor(xmatch, xi[:].unsqueeze(2).broadcast_to([P, NG, NXI, TOPK]),
                                con("xno").rearrange("p (i a) -> p i a", a=TOPK).unsqueeze(1).broadcast_to([P, NG, NXI, TOPK]), ALU.is_equal).then_inc(S["xmatch_ready"], 1)

            for t in range(NT):
                rope(t)
                if t == 0:
                    dve.wait_ge(S["zexp_ready"], 1)
                    v.tensor_scalar(beta, beta, 1.0, None, ALU.add).then_inc(S["zden_ready"], 1)
                    dve.wait_ge(S["zden_ready"], 1)
                    v.reciprocal(beta, beta).then_inc(S["zrec_ready"], 1)
                    dve.wait_ge(S["zrec_ready"], 1)
                    v.tensor_scalar(beta, beta, BETA_MIN, BETA_MAX, ALU.max, ALU.min).then_inc(S["beta_ready"], 1)
                if t == 2:
                    dve.wait_ge(S["betaT_done"], 1)
                    v.tensor_copy(betaT, bank[5][:, 0:P]).then_inc(S["betaT_ready"], 1)
                    dve.wait_ge(S["betaT_ready"], 1)
                    v.tensor_tensor_scan(decT, betaT, betaT, 1.0, ALU.mult, ALU.min).then_inc(S["decT_ready"], 1)
                    dve.wait_ge(S["decT_ready"], 1)
                    v.tensor_scalar(endcol[:], con("chunkcol"), decT[:, P - 1:P], None, ALU.mult).then_inc(S["endcol_ready"], 1)
                    dve.wait_ge(S["endcol_ready"], 1)
                    v.reciprocal(decT, decT).then_inc(S["rdecT_ready"], 1)
                if t == 5:
                    dve.wait_ge(S["rdec_done"], 1)
                    v.tensor_copy(rdec[:].rearrange("p t h -> p (t h)"), bank[3][:, 0:P]).then_inc(S["rdec_ready"], 1)
                    dve.wait_ge(S["enddec_done"], 1)
                    v.tensor_copy(enddec[:].rearrange("p k t -> p (k t)"), bank[4][:, 0:HG * NT]).then_inc(S["enddec_ready"], 1)
                if t == 1:
                    split_weights(dve, v, 3)
                if t >= 2:
                    feature(t - 2)
                if t == 3:
                    choose_pairs()
                if t == 6:
                    count_pairs()
            feature(NT - 2)
            feature(NT - 1)
            mlp(0)

            def rank_y(n):
                gs = slice(n * RANKED, (n + 1) * RANKED)
                if n == 0:
                    dve.wait_ge(S["bf_consts"], 4)
                    dve.wait_ge(S["xi_ready"], 2)
                else:
                    dve.wait_ge(S["yrank_steps"], 4 * n)
                v.tensor_tensor(ymatch, yi[:, gs, :].unsqueeze(2).broadcast_to([P, RANKED, NKEY, TOPK]),
                                keyno[:].unsqueeze(1).broadcast_to([P, RANKED, NKEY, TOPK]), ALU.is_equal).then_inc(S["ymatch_ready"], 1)
                dve.wait_ge(S["ymatch_ready"], n + 1)
                ym = ymatch.rearrange("p g j b -> p (g j) b")
                v.tensor_tensor(ym, ym, rankweight[:].unsqueeze(1).broadcast_to([P, RANKED * NKEY, TOPK]), ALU.mult).then_inc(S["yrank_steps"], 1)
                dve.wait_ge(S["yrank_steps"], 4 * n + 1)
                y4 = yt4.rearrange("p g j b -> p (g j) b")
                v.tensor_tensor(y4, ym[:, :, 0:4], ym[:, :, 4:8], ALU.add).then_inc(S["yrank_steps"], 1)
                dve.wait_ge(S["yrank_steps"], 4 * n + 2)
                v.tensor_tensor(ym[:, :, 0:2], y4[:, :, 0:2], y4[:, :, 2:4], ALU.add).then_inc(S["yrank_steps"], 1)
                dve.wait_ge(S["yrank_steps"], 4 * n + 3)
                v.tensor_tensor(yrank[:, gs, :].rearrange("p g j -> p (g j)"), ym[:, :, 0], ym[:, :, 1], ALU.add).then_inc(S["yrank_steps"], 1)

            def sums():
                dve.wait_ge(S["psel_ready"], 1)
                v.tensor_reduce(rowsum[:], pair.rearrange("p g (a b) -> p g a b", b=TOPK), AX.X, ALU.add).then_inc(S["rowsum_ready"], 1)
                dve.wait_ge(S["rowsum_ready"], 1)
                v.tensor_reduce(total[:], rowsum[:], AX.X, ALU.add).then_inc(S["total_ready"], 1)
                dve.wait_ge(S["total_ready"], 1)
                v.scalar_tensor_tensor(beyond[:], xi[:], float(NXI), rowsum[:], ALU.is_ge, ALU.mult).then_inc(S["beyond_ready"], 1)
                v.reciprocal(rtotal[:], total[:]).then_inc(S["rtotal_ready"], 1)
                dve.wait_ge(S["beyond_ready"], 1)
                v.tensor_reduce(beyond1[:], beyond[:], AX.X, ALU.add).then_inc(S["beyond1_ready"], 1)
                dve.wait_ge(S["xmatchc_ready"], 1)
                v.tensor_reduce(xcount[:], xmatch, AX.X, ALU.add).then_inc(S["xcount_ready"], 1)
                dve.wait_ge(S["xcount_ready"], 1)
                v.tensor_scalar(xcount[:], xcount[:], -1.0, float(TOPK), ALU.mult, ALU.add).then_inc(S["xlimit_ready"], 1)
                dve.wait_ge(S["rtotal_ready"], 1)
                dve.wait_ge(S["beyond1_ready"], 1)
                v.tensor_tensor(beyond1[:], beyond1[:], rtotal[:], ALU.mult).then_inc(S["beyond1_ready"], 1)

            def prob_mask(g):
                dve.wait_ge(S["xlimit_ready"], 1)
                dve.wait_ge(S["yrank_steps"], 4 * (g // RANKED + 1))
                if g < GPH:
                    for w in (-2, -1):
                        wait_split(dve, len(staged) + w)
                else:
                    dve.wait_ge(S["pT_done"], g - GPH + 1)
                v.tensor_tensor(prob[:, g % GPH], yrank[:, g].unsqueeze(1).broadcast_to([P, NXI, NKEY]),
                                xcount[:, g].unsqueeze(2).broadcast_to([P, NXI, NKEY]), ALU.is_gt).then_inc(S["prob0_ready"], 1)

            def copy_round(c, r):
                dve.wait_ge(S["t_done"], 4 * c + r + 1)
                if c >= 1:
                    dve.wait_ge(S["s_done"], 4 * (c - 1) + 2 * (r // 2) + 2)
                v.tensor_copy(qk4[:, r], bank[5][:].rearrange("p (w i n) -> p w i n", w=2, i=2)).then_inc(S["t_ready_dve"], 1)

            def mask(c, unit):
                if unit == 0 and c >= 1:
                    dve.wait_ge(S["y_done"], c)
                for odd in range(2):
                    dve.wait_ge(S["s_done"], 4 * c + 2 * unit + odd + 1)
                    v.tensor_tensor(sc[:, unit, odd], bank[3 + odd][:].rearrange("p (i n) -> p i n", n=P),
                                    causal[:].unsqueeze(1).broadcast_to([P, 4, P]), ALU.mult).then_inc(S["sc_ready"], 1)

            def chunk_sum(c):
                dve.wait_ge(S["u_done"], c + 1)
                dve.wait_ge(S["enddec_ready"], 1)
                if c >= 1:
                    dve.wait_ge(S["state_ready"], 2 * c)
                for hg in range(HG):
                    v.scalar_tensor_tensor(upd[:, hg], bank[7][:, hg * HPG * E1:(hg + 1) * HPG * E1], enddec[:, hg, c:c + 1],
                                           headblock[:], ALU.mult, ALU.mult).then_inc(S["upd_ready"], 1)

            def advance_state(c):
                for hg in range(HG):
                    dve.wait_ge(S["upd_ready"], 2 * c + hg + 1)
                    if c == 0:
                        v.tensor_copy(state[:, hg], upd[:, hg]).then_inc(S["state_ready"], 1)
                    else:
                        v.scalar_tensor_tensor(state[:, hg], state[:, hg], enddec[:, hg, c:c + 1], upd[:, hg], ALU.mult, ALU.add).then_inc(S["state_ready"], 1)

            def normalise(c):
                yb = bank[6][:, 0:HEADS * E1].rearrange("p (h e) -> p h e", e=E1)
                dve.wait_ge(S["y_done"], c + 1)
                v.scalar_tensor_tensor(den[:], rdec[:, c, :], EPS_DEN, yb[:, :, D], ALU.mult, ALU.add).then_inc(S["den_ready"], 1)
                dve.wait_ge(S["den_ready"], c + 1)
                v.reciprocal(rden[:], den[:]).then_inc(S["rden_ready"], 1)
                dve.wait_ge(S["rden_ready"], c + 1)
                if c == 0:
                    dve.wait_ge(S["psel_ready"], 1)
                if c >= 1:
                    dve.wait_ge(S["yT_done"], c)
                v.tensor_tensor(y, yb[:, :, 0:D], rden[:].unsqueeze(2).broadcast_to([P, HEADS, D]), ALU.mult).then_inc(S["y_ready"], 1)

            def yT_lo(c):
                dve.wait_ge(S["yT_hi"], c + 1)
                at = (c % CPH) * P
                v.tensor_tensor(yT[:, LO, :, at:at + P], bank[7][:, 0:HID].rearrange("p (k n) -> p k n", k=HG), yT[:, HI, :, at:at + P].bitcast(F32),
                                ALU.subtract).then_inc(S["yT_lo"], 1)

            def finish(g):
                dve.wait_ge(S["fin_done"], g + 1)
                dve.wait_ge(S["xb_ready"], g // 2 + 1)
                v.tensor_tensor(fin[:, g], place_bank(fin_place(g))[:, 0:HID], fin[:, g], ALU.add).then_inc(S["fin_ready"], 1)

            def coef_product(g):
                dve.wait_ge(S["pT_done"], g + 1)
                dve.wait_ge(S["h_ready"], (g // GPH + 1) * EC)
                hg_ = hT[:, :, group_cols(g, HT)]
                v.tensor_tensor(hg_, bank[3 + g % 2][:].rearrange("p (e n) -> p e n", n=P), hg_, ALU.mult).then_inc(S["coefprod_ready"], 1)

            def coef_lo(g):
                dve.wait_ge(S["coef_hi"], g + 1)
                if g % GPH >= 2:
                    dve.wait_ge(S["fin_done"], g - 1)
                v.tensor_tensor(coef[:, g % 2, LO], hT[:, :, group_cols(g, HT)], coef[:, g % 2, HI].bitcast(F32), ALU.subtract).then_inc(S["coef_lo"], 1)

            def attention(H, q):
                for c, step in steps(H, q):
                    if step == 4:
                        mask(c, 1)
                    if step == 5:
                        normalise(c)
                        if c < NT - 1:
                            advance_state(c)
                    if step == 7:
                        yT_lo(c)
                for c, step in steps(H, q):
                    if step == 1:
                        copy_round(c, 1)
                    if step == 3:
                        copy_round(c, 3)
                    if step == 2:
                        mask(c, 0)
                        if c < NT - 1:
                            chunk_sum(c)

            match_x()
            for H in range(HALVES):
                for q in range(START[0] if H == 0 else 0, PIECES):
                    if q < 2 * MC and q % 2 == 1:
                        mlp(H * MC + q // 2)
                    attention(H, q)
                    if H == 0:
                        if q in (4, 6, 8, 10):
                            split_weights(dve, v, 2 + q // 2)
                        if q in (6, 7, 15, 16):
                            rank_y((6, 7, 15, 16).index(q))
                        if q == 9:
                            sums()
                        if q in (12, 13, 16, 17):
                            prob_mask((12, 13, 16, 17).index(q))
                    elif q in (2, 4, 6, 8):
                        prob_mask(GPH + q // 2 - 1)
                dve.wait_ge(S["prob_ready"], (H + 1) * GPH)
                dve.wait_ge(S["beyond1_ready"], 2)
                v.tensor_tensor(prob[:, :, NXI - 1, NKEY - 1], prob[:, :, NXI - 1, NKEY - 1], beyond1[:, H * GPH:(H + 1) * GPH], ALU.add).then_inc(S["beyond2_ready"], 1)
                for g in range(H * GPH, (H + 1) * GPH):
                    coef_product(g)
                    attention(H, PIECES + g % GPH)
                    if g > H * GPH:
                        finish(g - 1)
                    coef_lo(g)
                finish((H + 1) * GPH - 1)


def constants():
    import numpy as np
    cols, n = const_columns()
    c = np.zeros((P, n), np.float32)

    def put(name, a):
        lo, hi = cols[name]
        c[:, lo:hi] = np.broadcast_to(np.asarray(a, np.float32).reshape(-1 if np.ndim(a) == 1 else P, *([] if np.ndim(a) == 1 else [-1])), (P, hi - lo))

    p = np.arange(P)
    put("ident", np.eye(P))
    put("causal", p[:, None] <= p[None, :])
    put("headblock", np.repeat(p[:, None] // D == np.arange(HPG)[None], E1, axis=1))
    half = D // 2
    inv_freq = np.float32(1.0) / np.float32(10000.0) ** (np.arange(half, dtype=np.float32) / np.float32(half))
    token = (np.arange(NT)[None, :] * P + p[:, None]).astype(np.float32) % np.float32(N_TOK)
    freqs = token[:, :, None] * inv_freq.astype(np.float32)
    put("cos", np.concatenate([np.cos(freqs)] * 2, axis=2).reshape(P, -1))
    put("sin", np.concatenate([np.sin(freqs), -np.sin(freqs)], axis=2).reshape(P, -1))
    put("keyno", np.repeat(np.arange(NKEY), TOPK))
    put("rankweight", TOPK - np.arange(TOPK))
    put("xno", np.repeat(np.arange(NXI), TOPK))
    put("chunkcol", p[:, None] // HEADS == np.arange(NT)[None])
    put("headrows", (p[:, None] % HEADS == (np.arange(HEADS).repeat(D))[None]))
    return c


_INS = ["L0_attn_x", "L0_attn_Wq", "L0_attn_Wk", "L0_attn_Wv", "L0_attn_Wg", "L0_attn_bg", "L0_attn_Wo", "L0_attn_bo",
        "L0_ffn_W_q", "L0_ffn_keys", "L0_ffn_down_embed", "L0_ffn_up_embed", "L0_ffn_gate_w", "L0_ffn_up_w", "L0_ffn_down_w"]


def kernel(**inputs):
    import numpy as np
    import concourse.bacc as bacc
    from concourse.bass_utils import run_bass_kernel_spmd

    nc = bacc.Bacc("TRN2", target_bir_lowering=False, num_devices=1)
    arrays, args = {}, []
    for name in _INS:
        a = np.ascontiguousarray(inputs[name])
        arrays[name] = a
        args.append(nc.dram_tensor(name, a.shape, mybir.dt.from_np(a.dtype), kind="ExternalInput").ap())
    arrays["constants"] = constants()
    args.append(nc.dram_tensor("constants", arrays["constants"].shape, F32, kind="ExternalInput").ap())
    out = nc.dram_tensor("out", (1, N_TOK, HID), F32, kind="ExternalOutput").ap()
    build(nc, *args, out)
    r = run_bass_kernel_spmd(nc, [arrays], core_ids=[0])
    return r.results[0]["out"]
```

```python
from contextlib import ExitStack

import concourse.bass as bass
from concourse import mybir

F32 = mybir.dt.float32
F32R = mybir.dt.float32r
BF16 = mybir.dt.bfloat16
U32 = mybir.dt.uint32
ALU = mybir.AluOpType
ACT = mybir.ActivationFunctionType
AX = mybir.AxisListType

P = 128
N_TOK = 1024
HID = 256
KC = HID // P
NT = N_TOK // P
NG = NT
HEADS = 16
D = HID // HEADS
E1 = D + 1
HG = 2
HPG = HEADS // HG
INTER = 1024
MC = INTER // P
NEXP = 512
EC = NEXP // P
NKEY = 64
TOPK = 8
NXI = NEXP // NKEY
EPS_DEN = 1e-6
EPS_LN = 1e-5
BETA_MIN, BETA_MAX = 0.8, 0.9995
MARK = -3.0e38
HALVES = 2
HT = N_TOK // HALVES
GPH = NG // HALVES
CPH = NT // HALVES
RANKED = 2
PIECES = 2 * MC + EC

HI, LO = 0, 1
PASSES = ((HI, HI), (HI, LO), (LO, HI))

CONST_PARTS = [("rankweight", TOPK), ("xno", NXI * TOPK), ("chunkcol", NT), ("ident", P), ("cos", NT * D), ("sin", NT * D),
               ("headrows", HG * P), ("causal", P), ("headblock", HPG * E1), ("keyno", NKEY * TOPK)]


def const_columns():
    at, out = 0, {}
    for name, n in CONST_PARTS:
        out[name] = (at, at + n)
        at += n
    return out, at


def build(nc, x, Wq, Wk, Wv, Wg, bg, Wo, bo, W_qr, keys, down_embed, up_embed, gate_w, up_w, down_w, consts, out):
    cols, n_const = const_columns()
    n_kept, n_rope, n_brief = cols["ident"][0], cols["headrows"][0], n_const - cols["headrows"][0]
    x_g = x.rearrange("a (t p j) d -> p (a t) (j d)", p=P, j=2)
    out_g = out.rearrange("a (t p j) d -> p (a t) (j d)", p=P, j=2)

    def rows(w):
        return w.rearrange("(k p) n -> p k n", p=P)

    with ExitStack() as ctx:
        def sb(name, shape, dt=F32):
            return ctx.enter_context(nc.sbuf_tensor(name, shape, dt))

        def sem(name):
            return ctx.enter_context(nc.semaphore(name))

        bank = [ctx.enter_context(nc.psum_tensor(f"bank{i}", [P, 512], F32)) for i in range(8)]

        xnT = sb("xnT", [P, 2, KC, N_TOK], F32R)
        gate_p = sb("gate_p", [P, 2, KC, INTER], F32R)
        up_p = sb("up_p", [P, 2, KC, INTER], F32R)
        down_p = sb("down_p", [P, 2, MC, HID], F32R)
        ue_p = sb("ue_p", [P, 2, EC, HID], F32R)
        deT = sb("deT", [P, 2, KC, NEXP], F32R)
        wo_p = sb("wo_p", [P, 2, KC, HID], F32R)
        yT = sb("yT", [P, 2, HG, HT], F32R)
        act_p = sb("act_p", [P, 2, MC, HT], F32R)
        early_p = act_p[:, :, :, :].rearrange("p s m n -> p s (m n)")
        ring = sb("ring", [P, 2048], F32R)
        qrT = ring[:, :].rearrange("p (s n) -> p s n", s=2)
        qk4 = ring[:, :].rearrange("p (r w i n) -> p r w i n", r=4, w=2, i=2)
        coef = ring[:, :].rearrange("p (b s e n) -> p b s e n", b=2, s=2, e=EC)
        qk_tok = sb("qk_tok", [P, 2, HEADS, 4, D], F32R)
        identr = sb("identr", [P, P], F32R)

        cst = sb("cst", [P, n_kept])
        causal = sb("causal", [P, P], BF16)
        headblock = sb("headblock", [P, HPG * E1], BF16)
        work = sb("work", [P, 2048])
        x_sb = work[:, :].rearrange("p (g n) -> p g n", g=NG)
        ROPES = 3
        ropeA = work[:, 512:2048].rearrange("p (b n) -> p b n", b=ROPES)
        pair = work[:, 0:512].rearrange("p (g n) -> p g n", g=NG)
        ymatch = work[:, 1024:1536].bitcast(BF16).rearrange("p (g j b) -> p g j b", g=RANKED, b=TOPK)
        xmatch = work[:, 1792:2048].bitcast(BF16).rearrange("p (g i a) -> p g i a", g=NG, a=TOPK)
        yt4 = work[:, 1536:1792].bitcast(BF16).rearrange("p (g j b) -> p g j b", g=RANKED, b=4)
        hT = work[:, :].rearrange("p (e n) -> p e n", e=EC)
        N_EARLY = KC * 2 * HID + KC * (HID + HEADS) + KC * P + 2 * 2 * NKEY
        early = sb("early", [P, N_EARLY])
        sc = early[:, 0:2048].rearrange("p (u s i n) -> p u s i n", u=2, s=2, i=4)

        WVG, WQR, KEYS, WQK = range(4)
        EARLY = ((KC, HID + HEADS), (KC, P), (2, 2 * NKEY), (KC, 2 * HID))

        def early_at(i):
            return sum(k * n for k, n in EARLY[:i])

        def early_w(i, part=None):
            k, n = EARLY[i]
            t = early if part is None else early_p[:, part]
            return t[:, early_at(i):early_at(i + 1)].rearrange("p (k n) -> p k n", k=k)

        prob = sb("prob", [P, GPH, NXI, NKEY])
        stage = prob[:, :, :, :].rearrange("p g i j -> p (g i j)").rearrange("p (s n) -> p s n", s=2)
        de_sb = sb("de_sb", [P, EC, HID])
        sil = de_sb[:, :, :].rearrange("p (u e) n -> p u (e n)", u=2)
        phi = sb("phi", [P, NT, 2 * HID])
        fin = phi[:, 0:NG // 2, :].rearrange("p t (j n) -> p (t j) n", j=2)
        v1 = sb("v1", [P, NT, HEADS, E1])
        xn = sb("xn", [P, 2, HID])
        chosen = xn[:, :, :].rearrange("p a n -> p (a n)").rearrange("p (g n) -> p g n", g=NG)
        qT = xn[:, 0, :].rearrange("p (k n) -> p k n", k=HG)
        y = xn[:, 1, :].rearrange("p (h d) -> p h d", d=D)
        stats = sb("stats", [P, NG, 6])
        mv = sb("mv", [P, NG, 2])
        std = sb("std", [P, NG])
        rstd = sb("rstd", [P, NG])
        bg_sb = sb("bg_sb", [P, HEADS])
        route = sb("route", [P, 2, NG, NKEY])
        tops = sb("tops", [P, HID])
        top = tops[:, 0:128].rearrange("p (s g n) -> p s g n", s=2, n=TOPK)
        topi = tops[:, 128:256].bitcast(U32).rearrange("p (s g n) -> p s g n", s=2, n=TOPK)
        bo_sb = tops[:, :]
        xi = sb("xi", [P, NG, TOPK])
        yi = sb("yi", [P, NG, TOPK], BF16)
        rowcount = sb("rowcount", [P, NG, TOPK])
        pair8 = sb("pair8", [P, NG, TOPK])
        rowsum = beyond = pair8
        total = sb("total", [P, NG])
        rtotal = sb("rtotal", [P, NG])
        xcount = sb("xcount", [P, NG, NXI])
        beyond1 = sb("beyond1", [P, NG])
        xw = sb("xw", [P, NG, NXI])
        yw = route[:, 1]
        upd = route[:, 0].rearrange("p g n -> p (g n)")[:, 0:HG * HPG * E1].rearrange("p (k n) -> p k n", k=HG)
        keyno = sb("keyno", [P, NKEY, TOPK], BF16)
        rankweight = sb("rankweight", [P, TOPK], BF16)
        etop = route[:, 0].rearrange("p g n -> p (g n)")[:, HG * HPG * E1:HG * HPG * E1 + 2 * NG * TOPK].rearrange("p (s g n) -> p s g n", s=2, n=TOPK)
        yrank = sb("yrank", [P, NG, NKEY])
        beta, betaT, decT = (yrank[:, 2 * i:2 * i + 2, :].rearrange("p g n -> p (g n)") for i in range(3))
        recur = sb("recur", [P, HG * HPG * E1])
        state = recur[:, :].rearrange("p (k n) -> p k n", k=HG)
        brief = phi[:, NT - 3:NT, :].rearrange("p t n -> p (t n)")[:, 0:n_brief]

        def con(name):
            a, b = cols[name]
            if b <= n_kept:
                return cst[:, a:b]
            if name == "ident":
                return yrank[:, 6:8, :].rearrange("p g n -> p (g n)")
            return recur[:, a - cols["cos"][0]:b - cols["cos"][0]] if b <= n_rope else brief[:, a - n_rope:b - n_rope]

        rdec = sb("rdec", [P, NT, HEADS])
        endcol = sb("endcol", [P, NT])
        enddec = sb("enddec", [P, HG, NT])
        den = sb("den", [P, HEADS])
        rden = sb("rden", [P, HEADS])

        ident = identr[:].bitcast(F32)

        START = (4, 1)

        def steps(H, q):
            return [(H * CPH + cl, q - START[H] - 4 * cl) for cl in range(CPH)]

        names = """x0_in x1_in x2_in x3_in consts_in ident_in route_in vg_in qk_in stage0_in stage1_in embed_in bg_in bo_in
            x_again0 x_again1 x_again2 x_again3 keys_zero v1_ones identr_ready stat_ready aggr_ready std_in std_ready
            rstd_ready xn_ready xnT_done xnT_hi xnT_lo route_w_hi route_w_lo early_hi v_w_lo qk_w_lo stage_hi
            stage0_lo stage1_lo qr_done qrT_hi qrT_lo route_done route_ready z_ready zb_ready zexp_ready zden_ready
            zrec_ready beta_ready betaT_done betaT_ready decT_ready rdecT_ready rdec_done rdec_ready endcol_ready
            enddec_done enddec_ready qk_done v_done v_ready ropeAB_ready rot_ready feat_in phi_ready kp_ready deT_done
            deT_hi deT_lo top_ready topi_ready xi_ready pair_ready pair8_ready marked_ready chosen_ready pexp_ready
            tdif_ready etop_ready wdif_ready xw_exp yw_exp psel_ready rowcount_ready rowsum_ready total_ready
            rtotal_ready bf_consts ymatch_ready yrank_steps xmatch_ready xmatchc_ready xcount_ready xlimit_ready
            beyond_ready beyond1_ready xw_ready prob0_ready prob1_ready prob_ready beyond2_ready tok_hi tok_lo t_done
            t_ready_act t_ready_dve qT_done qT_ready s_done sc_ready u_done upd_ready state_ready y_done den_ready
            rden_ready y_ready yT_done yT_hi yT_lo gate_done up_done silu_ready mlp_ready act_hi act_lo h_done h_ready
            pT_done coefprod_ready coef_hi coef_lo fin_done xb_ready fin_ready out_done""".split()
        S = {n: sem(n) for n in names}

        block = ctx.enter_context(nc.Block())

        def group_cols(g, within=N_TOK):
            T, j = divmod(g % (2 * within // (2 * P)), 2)
            return slice(T * 2 * P + j, (T + 1) * 2 * P - 1 + j, 2)

        PLACES = PIECES + GPH

        def gate_place(u):
            return (u // MC) * PLACES + 2 * (u % MC)

        def h_place(v):
            return (v // EC) * PLACES + 2 * MC + v % EC

        def fin_place(g):
            return (g // GPH) * PLACES + PIECES + g % GPH

        def place_bank(n):
            return bank[3 + n] if n < 2 else bank[(n - 2) % 3]

        def wait_place_free(eng, n):
            if n < 5:
                return
            H, q = divmod(n - 3, PLACES)
            if q < 2 * MC and q % 2 == 0:
                eng.wait_ge(S["silu_ready"], H * MC + q // 2 + 1)
            elif q < 2 * MC:
                eng.wait_ge(S["mlp_ready"], H * MC + q // 2 + 1)
            elif q < PIECES:
                eng.wait_ge(S["h_ready"], H * EC + q - 2 * MC + 1)
            else:
                eng.wait_ge(S["fin_ready"], H * GPH + q - PIECES + 1)

        def stage_items():
            for w, dst in ((gate_w, gate_p), (up_w, up_p)):
                for k in range(KC):
                    yield w[k * P:(k + 1) * P, :], INTER, dst[:, :, k, :]
            for i in range(2):
                yield rows(down_w)[:, 4 * i:4 * i + 4, :], 1024, down_p[:, :, 4 * i:4 * i + 4, :].rearrange("p s m n -> p s (m n)")
            yield rows(up_embed), 1024, ue_p[:, :, :, :].rearrange("p s m n -> p s (m n)")
            yield rows(Wo), 512, wo_p[:, :, :, :].rearrange("p s m n -> p s (m n)")

        staged = list(stage_items())

        def wait_split(eng, w):
            eng.wait_ge(S[f"stage{w % 2}_lo"], w // 2 + 1)

        def split_weights(eng, ops, w):
            _src, n, dst = staged[w]
            eng.wait_ge(S["stage_hi"], w + 1)
            ops.tensor_tensor(dst[:, LO], stage[:, w % 2, 0:n], dst[:, HI].bitcast(F32), ALU.subtract).then_inc(S[f"stage{w % 2}_lo"], 1)

        @block.sync
        def _(sp):
            for T in range(NG // 2):
                sp.dma_start(x_sb[:, 2 * T:2 * T + 2, :].rearrange("p j d -> p (j d)"), x_g[:, T, :]).then_inc(S[f"x{T}_in"], 16)
            sp.dma_start(early_w(WQR), rows(W_qr)).then_inc(S["route_in"], 16)
            sp.wait_ge(S["keys_zero"], 1)
            for half in range(2):
                for j in range(2):
                    sp.dma_start(early_w(KEYS)[64 * j:64 * j + 64, half, NKEY * j:NKEY * j + NKEY], keys[half]).then_inc(S["route_in"], 16)
            sp.dma_start(early_w(WVG)[:, :, 0:HID], rows(Wv)).then_inc(S["vg_in"], 16)
            sp.dma_start(early_w(WVG)[:, :, HID:HID + HEADS], rows(Wg)).then_inc(S["vg_in"], 16)
            sp.dma_start(early_w(WQK)[:, :, 0:HID], rows(Wq)).then_inc(S["qk_in"], 16)
            sp.dma_start(early_w(WQK)[:, :, HID:2 * HID], rows(Wk)).then_inc(S["qk_in"], 16)
            for w, (src, n, _dst) in enumerate(staged):
                if w == 1:
                    sp.dma_start(de_sb[:], rows(down_embed)).then_inc(S["embed_in"], 16)
                if w >= 2:
                    wait_split(sp, w - 2)
                dst = stage[:, w % 2, 0:n]
                if w >= 4:
                    dst = dst.rearrange("p (m n) -> p m n", n=HID)
                sp.dma_start(dst, src).then_inc(S[f"stage{w % 2}_in"], 16)
            sp.wait_ge(S["xi_ready"], 2)
            sp.wait_ge(S["wdif_ready"], 2)
            sp.dma_start(bo_sb, bo.rearrange("(a n) -> a n", a=1).broadcast_to([P, HID])).then_inc(S["bo_in"], 16)
            for T in range(NG // 2):
                if T >= 1:
                    sp.wait_ge(S["qT_done"], T)
                sp.wait_ge(S["u_done"], T + 1)
                sp.wait_ge(S["tok_lo"], 4 * T + 4)
                sp.dma_start(phi[:, T, :], x_g[:, T, :]).then_inc(S[f"x_again{T}"], 16)
            for T in range(NG // 2):
                sp.wait_ge(S["fin_ready"], 2 * T + 2)
                sp.dma_start(out_g[:, T, :], phi[:, T, :]).then_inc(S["out_done"], 16)
            sp.wait_ge(S["out_done"], 16 * (NG // 2))

        def tok_parts(c, unit, which):
            src = phi[:, c, which * HID + unit * P:which * HID + (unit + 1) * P].rearrange("p (h d) -> p h d", d=D)
            dst = qk_tok[:, which, unit * HPG:(unit + 1) * HPG, :, :]
            twice = src.unsqueeze(2).broadcast_to([P, HPG, 2, D])
            if which == 0:
                return twice, dst[:, :, 0:4:2, :], dst[:, :, 1:4:2, :]
            return twice, dst[:, :, 0:2, :], dst[:, :, 2:4, :]

        @block.gpsimd
        def _(pool):
            g = nc.gpsimd
            g.dma_start(cst[:], consts[:, 0:n_kept]).then_inc(S["consts_in"], 16)
            g.dma_start(brief, consts[:, n_rope:n_const]).then_inc(S["consts_in"], 16)
            g.dma_start(recur[:, 0:n_rope - cols["cos"][0]], consts[:, cols["cos"][0]:n_rope]).then_inc(S["consts_in"], 16)
            g.dma_start(bg_sb[:], bg.rearrange("(a n) -> a n", a=1).broadcast_to([P, HEADS])).then_inc(S["bg_in"], 16)
            g.memset(early_w(KEYS), 0.0).then_inc(S["keys_zero"], 1)
            g.memset(v1[:], 1.0).then_inc(S["v1_ones"], 1)

            def rotate(t):
                pool.wait_ge(S["ropeAB_ready"], 2 * t + 2)
                a, b = (z.rearrange("p (h s d) -> p h s d", s=2, d=D // 2) for z in (ropeA[:, t % ROPES], phi[:, t]))
                for s in range(2):
                    g.tensor_tensor(a[:, :, s, :], a[:, :, s, :], b[:, :, 1 - s, :], ALU.add).then_inc(S["rot_ready"], 1)

            def key_scale(t):
                pool.wait_ge(S["phi_ready"], t + 1)
                pool.wait_ge(S["rdec_ready"], 1)
                kk = phi[:, t, HID:2 * HID].rearrange("p (h d) -> p h d", d=D)
                g.tensor_tensor(kk, kk, rdec[:, t].unsqueeze(2).broadcast_to([P, HEADS, D]), ALU.mult).then_inc(S["kp_ready"], 1)

            def tok_lo(c, unit):
                pool.wait_ge(S["tok_hi"], 4 * c + 2 * unit + 2)
                for which in range(2):
                    twice, hi, lo = tok_parts(c, unit, which)
                    g.tensor_tensor(lo, twice, hi.bitcast(F32), ALU.subtract).then_inc(S["tok_lo"], 1)

            def act_lo(u):
                pool.wait_ge(S["act_hi"], u + 1)
                g.tensor_tensor(act_p[:, LO, u % MC, :], sil[:, u % 2], act_p[:, HI, u % MC, :].bitcast(F32), ALU.subtract).then_inc(S["act_lo"], 1)

            def pair_sums():
                for side in range(2):
                    pool.wait_ge(S["top_ready"], NG * side + NG)
                g.tensor_tensor(pair.rearrange("p g (a b) -> p g a b", b=TOPK),
                                top[:, 0].unsqueeze(3).broadcast_to([P, NG, TOPK, TOPK]),
                                top[:, 1].unsqueeze(2).broadcast_to([P, NG, TOPK, TOPK]), ALU.add).then_inc(S["pair_ready"], 1)

            def weight_exponents():
                pool.wait_ge(S["topi_ready"], 2 * NG)
                g.tensor_tensor(xw[:], route[:, 0, :, 0:NXI], top[:, 0, :, 0:1].broadcast_to([P, NG, NXI]), ALU.subtract).then_inc(S["wdif_ready"], 1)
                g.tensor_tensor(yw, yw, top[:, 1, :, 0:1].broadcast_to([P, NG, NKEY]), ALU.subtract).then_inc(S["wdif_ready"], 1)
                pool.wait_ge(S["wdif_ready"], 1)
                g.tensor_tensor(etop, top, top[:, :, :, 0:1].broadcast_to([P, 2, NG, TOPK]), ALU.subtract).then_inc(S["tdif_ready"], 1)

            def weigh_pairs():
                pool.wait_ge(S["etop_ready"], 1)
                pool.wait_ge(S["marked_ready"], NG)
                g.tensor_tensor(pair.rearrange("p g (a b) -> p g a b", b=TOPK),
                                etop[:, 0].unsqueeze(3).broadcast_to([P, NG, TOPK, TOPK]),
                                etop[:, 1].unsqueeze(2).broadcast_to([P, NG, TOPK, TOPK]), ALU.mult).then_inc(S["pexp_ready"], 1)
                pool.wait_ge(S["chosen_ready"], 1)
                pool.wait_ge(S["pexp_ready"], 1)
                g.tensor_tensor(pair, pair, chosen, ALU.mult).then_inc(S["psel_ready"], 1)
                pool.wait_ge(S["xmatch_ready"], 1)
                pool.wait_ge(S["rowcount_ready"], 1)
                g.tensor_tensor(xmatch, xmatch, rowcount[:].unsqueeze(2).broadcast_to([P, NG, NXI, TOPK]), ALU.mult).then_inc(S["xmatchc_ready"], 1)

            def scale_xw():
                pool.wait_ge(S["xw_exp"], 1)
                pool.wait_ge(S["rtotal_ready"], 1)
                g.tensor_tensor(xw[:], xw[:], rtotal[:].unsqueeze(2).broadcast_to([P, NG, NXI]), ALU.mult).then_inc(S["xw_ready"], 1)

            def probabilities(q):
                b = q % GPH
                pool.wait_ge(S["prob0_ready"], q + 1)
                pool.wait_ge(S["yw_exp"], 1)
                g.tensor_tensor(prob[:, b], prob[:, b], yw[:, q].unsqueeze(1).broadcast_to([P, NXI, NKEY]), ALU.mult).then_inc(S["prob1_ready"], 1)
                pool.wait_ge(S["prob1_ready"], q + 1)
                pool.wait_ge(S["xw_ready"], 1)
                g.tensor_tensor(prob[:, b], prob[:, b], xw[:, q].unsqueeze(2).broadcast_to([P, NXI, NKEY]), ALU.mult).then_inc(S["prob_ready"], 1)

            pool.wait_ge(S["route_w_hi"], 1)
            at = slice(early_at(WQR), early_at(WQK))
            g.tensor_tensor(early_p[:, LO, at], early[:, at], early_p[:, HI, at].bitcast(F32), ALU.subtract).then_inc(S["route_w_lo"], 1)
            pool.wait_ge(S["early_hi"], 1)
            at_v = slice(early_at(WVG), early_at(WVG + 1))
            g.tensor_tensor(early_p[:, LO, at_v], early[:, at_v], early_p[:, HI, at_v].bitcast(F32), ALU.subtract).then_inc(S["v_w_lo"], 1)
            split_weights(pool, g, 0)
            split_weights(pool, g, 2)
            pair_sums()
            for t in range(NT):
                rotate(t)
                if t == 1:
                    weight_exponents()
                if t == 4:
                    key_scale(0)
                if t == 5:
                    tok_lo(0, 0)
                if t == 7:
                    tok_lo(0, 1)
            act_lo(0)
            key_scale(1)
            act_lo(1)
            for H in range(HALVES):
                for q in range(START[0] if H == 0 else 0, PIECES):
                    if q < 2 * MC and q % 2 == 1:
                        act_lo(H * MC + q // 2)
                    for c, step in steps(H, q):
                        if step == 0 and c + 2 < NT:
                            key_scale(c + 2)
                        if step in (1, 3) and c + 1 < NT:
                            tok_lo(c + 1, step // 2)
                    if H == 0:
                        if q == 6:
                            weigh_pairs()
                        if q in (7, 12):
                            split_weights(pool, g, 5 if q == 7 else 7)
                        if q == 10:
                            scale_xw()
                        if q in (14, 15, 16, 18):
                            probabilities((14, 15, 16, 18).index(q))
                    elif q in (6, 8, 10, 12):
                        probabilities(q // 2 + 1)
                    if (H, q) in ((0, 15), (0, 19), (1, 1), (1, 3)):
                        T = 2 * H + (q % 15 >= 3)
                        pool.wait_ge(S[f"x_again{T}"], 16)
                        pool.wait_ge(S["bo_in"], 16)
                        g.tensor_tensor(fin[:, 2 * T:2 * T + 2], fin[:, 2 * T:2 * T + 2], bo_sb.unsqueeze(1).broadcast_to([P, 2, HID]), ALU.add).then_inc(S["xb_ready"], 1)

        @block.scalar
        def _(act):
            a = nc.scalar
            a.dma_start(con("ident"), consts[:, cols["ident"][0]:cols["ident"][1]]).then_inc(S["ident_in"], 16)
            def root(T):
                act.wait_ge(S["std_in"], T + 1)
                a.activation(std[:, 2 * T:2 * T + 2], std[:, 2 * T:2 * T + 2], ACT.Sqrt).then_inc(S["std_ready"], 1)

            root(0)
            act.wait_ge(S["ident_in"], 16)
            a.activation(identr[:], con("ident"), ACT.Copy).then_inc(S["identr_ready"], 1)
            root(1)
            root(2)

            def early_hi(i, j, when, count, event):
                act.wait_ge(S[when], count)
                at = slice(early_at(i), early_at(j))
                a.activation(early_p[:, HI, at], early[:, at], ACT.Copy).then_inc(S[event], 1)

            def xnT_hi(g):
                act.wait_ge(S["xnT_done"], g + 1)
                a.activation(xnT[:, HI, :, group_cols(g)], bank[g % 3][:, 0:2 * P].rearrange("p (k n) -> p k n", k=KC), ACT.Copy).then_inc(S["xnT_hi"], 1)

            def qrT_hi(half):
                act.wait_ge(S["qr_done"], half + 1)
                a.activation(qrT[:, HI, half * 512:half * 512 + 512], bank[3 + half][:], ACT.Copy).then_inc(S["qrT_hi"], 1)

            def copy_route(half):
                act.wait_ge(S["route_done"], half + 1)
                a.activation(route[:, half].rearrange("p g n -> p (g n)"), bank[(5, 3)[half]][:], ACT.Copy).then_inc(S["route_ready"], 1)

            def copy_v(t):
                act.wait_ge(S["v_done"], t + 1)
                b = bank[6 + t % 2]
                a.activation(v1[:, t, :, 0:D], b[:, 0:HID].rearrange("p (h d) -> p h d", d=D), ACT.Copy).then_inc(S["v_ready"], 1)
                a.activation(beta[:, t * HEADS:(t + 1) * HEADS], b[:, HID:HID + HEADS], ACT.Copy).then_inc(S["z_ready"], 1)

            def weights_hi(w):
                _src, n, dst = staged[w]
                act.wait_ge(S[f"stage{w % 2}_in"], 16 * (w // 2 + 1))
                a.activation(dst[:, HI], stage[:, w % 2, 0:n], ACT.Copy).then_inc(S["stage_hi"], 1)

            def tok_hi(c, unit):
                act.wait_ge(S["kp_ready"], c + 1)
                if c >= 1:
                    act.wait_ge(S["t_done"], 4 * (c - 1) + 2 * unit + 2)
                for which in range(2):
                    twice, hi, _lo = tok_parts(c, unit, which)
                    a.activation(hi, twice, ACT.Copy).then_inc(S["tok_hi"], 1)

            def silu(u):
                act.wait_ge(S["gate_done"], u + 1)
                if u >= 2:
                    act.wait_ge(S["act_lo"], u - 1)
                a.activation(sil[:, u % 2], place_bank(gate_place(u))[:], ACT.Silu).then_inc(S["silu_ready"], 1)

            def copy_round(c, r):
                act.wait_ge(S["t_done"], 4 * c + r + 1)
                if c >= 1:
                    act.wait_ge(S["s_done"], 4 * (c - 1) + 2 * (r // 2) + 2)
                if c == CPH and r == 0:
                    act.wait_ge(S["fin_done"], GPH)
                a.activation(qk4[:, r], bank[5][:].rearrange("p (w i n) -> p w i n", w=2, i=2), ACT.Copy).then_inc(S["t_ready_act"], 1)

            def act_hi(u):
                act.wait_ge(S["mlp_ready"], u + 1)
                a.activation(act_p[:, HI, u % MC, :], sil[:, u % 2], ACT.Copy).then_inc(S["act_hi"], 1)

            xnT_hi(0)
            xnT_hi(1)
            root(3)
            early_hi(WQR, WQK, "route_in", 80, "route_w_hi")
            xnT_hi(2)
            xnT_hi(3)
            early_hi(WVG, WQR, "vg_in", 32, "early_hi")
            xnT_hi(4)
            xnT_hi(5)
            early_hi(WQK, WQK + 1, "qk_in", 32, "early_hi")
            xnT_hi(6)
            xnT_hi(7)
            weights_hi(0)
            qrT_hi(0)
            qrT_hi(1)
            weights_hi(1)
            act.wait_ge(S["v1_ones"], 1)
            copy_v(0)
            copy_v(1)
            copy_route(0)
            copy_v(2)
            copy_v(3)
            copy_route(1)
            copy_v(4)
            copy_v(5)
            weights_hi(2)
            copy_v(6)
            copy_v(7)
            act.wait_ge(S["zb_ready"], 1)
            a.activation(beta, beta, ACT.Exp, scale=-1.0).then_inc(S["zexp_ready"], 1)
            for k in range(KC):
                act.wait_ge(S["deT_done"], k + 1)
                a.activation(deT[:, HI, k], bank[(4, 5)[k]][:], ACT.Copy).then_inc(S["deT_hi"], 1)
            weights_hi(3)
            def features(t):
                act.wait_ge(S["rot_ready"], 2 * t + 2)
                a.activation(phi[:, t], ropeA[:, t % ROPES], ACT.Relu).then_inc(S["feat_in"], 1)
                a.activation(ropeA[:, t % ROPES], ropeA[:, t % ROPES], ACT.Exp).then_inc(S["feat_in"], 1)

            for t in range(NT - 1):
                features(t)
                if t == 2:
                    act.wait_ge(S["wdif_ready"], 2)
                    a.activation(xw[:], xw[:], ACT.Exp).then_inc(S["xw_exp"], 1)
                    a.activation(yw, yw, ACT.Exp).then_inc(S["yw_exp"], 1)
                    act.wait_ge(S["tdif_ready"], 1)
                    a.activation(etop, etop, ACT.Exp).then_inc(S["etop_ready"], 1)
                if t == 4:
                    tok_hi(0, 0)
                    tok_hi(0, 1)
            silu(0)
            silu(1)
            copy_round(0, 0)
            features(NT - 1)
            act_hi(0)
            act_hi(1)
            def copy_qT(c):
                act.wait_ge(S["qT_done"], c)
                a.activation(qT, bank[7][:, 0:HID].rearrange("p (k n) -> p k n", k=HG), ACT.Copy).then_inc(S["qT_ready"], 1)

            def yT_hi(c):
                act.wait_ge(S["yT_done"], c + 1)
                at = (c % CPH) * P
                a.activation(yT[:, HI, :, at:at + P], bank[7][:, 0:HID].rearrange("p (k n) -> p k n", k=HG), ACT.Copy).then_inc(S["yT_hi"], 1)

            def coef_hi(g):
                act.wait_ge(S["coefprod_ready"], g + 1)
                if g % GPH >= 2:
                    act.wait_ge(S["fin_done"], g - 1)
                a.activation(coef[:, g % 2, HI], hT[:, :, group_cols(g, HT)], ACT.Copy).then_inc(S["coef_hi"], 1)

            def attention(H, q):
                for c, step in steps(H, q):
                    if step == 0:
                        copy_round(c, 0)
                    if step == 2:
                        copy_round(c, 2)
                    if step == 4 and c >= 1:
                        copy_qT(c)
                    if step == 6:
                        yT_hi(c)
                for c, step in steps(H, q):
                    if step in (1, 3) and c + 1 < NT:
                        tok_hi(c + 1, step // 2)

            for H in range(HALVES):
                for q in range(START[0] if H == 0 else 0, PIECES):
                    if q < 2 * MC and q % 2 == 0:
                        silu(H * MC + q // 2)
                    elif q >= 2 * MC:
                        v = H * EC + q - 2 * MC
                        act.wait_ge(S["h_done"], v + 1)
                        if v == 0:
                            act.wait_ge(S["psel_ready"], 1)
                            act.wait_ge(S["rowsum_ready"], 1)
                        if v == 2:
                            act.wait_ge(S["yrank_steps"], 4 * (NG // RANKED))
                        a.activation(hT[:, v % EC, :], place_bank(h_place(v))[:], ACT.Silu).then_inc(S["h_ready"], 1)
                    if (H, q) != (0, START[0]):
                        attention(H, q)
                    if q < 2 * MC and q % 2 == 1:
                        act_hi(H * MC + q // 2)
                    if H == 0 and q in (4, 6, 8, 11):
                        weights_hi(4 + (4, 6, 8, 11).index(q))
                attention(H, PIECES)
                for i in range(GPH):
                    coef_hi(H * GPH + i)
                    attention(H, PIECES + i + 1)

        @block.tensor
        def _(pe):
            t_ = nc.tensor

            def product(out_, pairs_, beside=None):
                n = len(pairs_) * len(PASSES)
                i = 0
                for lhs, rhs in pairs_:
                    for a, b in PASSES:
                        mm = t_.matmul(out_, lhs(a), rhs(b), start=i == 0, stop=i == n - 1)
                        i += 1
                        if beside is not None and i < n:
                            beside(i - 1)
                return mm

            def gate_or_up(u, w_p, n, event, beside=None):
                m, half = u % MC, u // MC
                if u == 0:
                    pe.wait_ge(S["xnT_lo"], NG)
                    for w in ((0, 1) if w_p is gate_p else (2, 3)):
                        wait_split(pe, w)
                wait_place_free(pe, n)
                product(place_bank(n)[:], [(lambda s, k=k: w_p[:, s, k, m * P:(m + 1) * P], lambda s, k=k: xnT[:, s, k, half * HT:(half + 1) * HT])
                                           for k in range(KC)], beside).then_inc(S[event], 1)

            PRELUDE = {t: (u, w_p, gate_place(u) + i, ("gate_done", "up_done")[i])
                       for t, (u, i, w_p) in zip((3, 4, 5, 6), ((0, 0, gate_p), (0, 1, up_p), (1, 0, gate_p), (1, 1, up_p)))}

            pe.wait_ge(S["identr_ready"], 1)

            def transpose_xn(g):
                pe.wait_ge(S["xn_ready"], g + 1)
                if g >= 3:
                    pe.wait_ge(S["xnT_lo"], g - 2)
                for k in range(KC):
                    mm = t_.transpose(bank[g % 3][:, k * P:(k + 1) * P], xn[:, g % 2, k * P:(k + 1) * P], ident)
                mm.then_inc(S["xnT_done"], 1)

            def queries(half):
                pe.wait_ge(S["route_w_lo"], 1)
                pe.wait_ge(S["xnT_lo"], 4 * half + 4)
                product(bank[3 + half][:], [(lambda s, k=k: early_w(WQR, s)[:, k, :], lambda s, k=k: xnT[:, s, k, half * 512:half * 512 + 512])
                                            for k in range(KC)]).then_inc(S["qr_done"], 1)

            def routing(half):
                pe.wait_ge(S["qrT_lo"], half + 1)
                for i in range(4):
                    c = (4 * half + i) * P
                    mm = product(bank[(5, 3)[half]][:, i * P:(i + 1) * P], [(lambda s: qrT[:, s, c:c + P], lambda s: early_w(KEYS, s)[:, half, :])])
                mm.then_inc(S["route_done"], 1)

            def v_and_z(t):
                if t == 0:
                    pe.wait_ge(S["v_w_lo"], 1)
                if t % 2 == 0:
                    pe.wait_ge(S["xnT_lo"], t + 2)
                if t >= 2:
                    pe.wait_ge(S["z_ready"], t - 1)
                product(bank[6 + t % 2][:, 0:HID + HEADS], [(lambda s, k=k: xnT[:, s, k, t * P:(t + 1) * P], lambda s, k=k: early_w(WVG, s)[:, k, :])
                                                            for k in range(KC)]).then_inc(S["v_done"], 1)

            for g in range(NG):
                transpose_xn(g)
            queries(0)
            queries(1)
            v_and_z(0)
            v_and_z(1)
            routing(0)
            v_and_z(2)
            v_and_z(3)
            routing(1)
            v_and_z(4)
            v_and_z(5)
            v_and_z(6)
            v_and_z(7)
            pe.wait_ge(S["embed_in"], 16)
            pe.wait_ge(S["route_ready"], 2)
            for k in range(KC):
                for e in range(EC):
                    mm = t_.transpose(bank[(4, 5)[k]][:, e * P:(e + 1) * P], de_sb[:, e, k * P:(k + 1) * P], ident)
                mm.then_inc(S["deT_done"], 1)
            pe.wait_ge(S["qk_w_lo"], 1)
            pe.wait_ge(S["z_ready"], NT)
            for t in range(NT):
                if t >= 2:
                    pe.wait_ge(S["ropeAB_ready"], 2 * (t - 1))
                product(bank[6 + t % 2][:], [(lambda s, k=k: xnT[:, s, k, t * P:(t + 1) * P], lambda s, k=k: early_w(WQK, s)[:, k, :])
                                             for k in range(KC)]).then_inc(S["qk_done"], 1)
                if t == 1:
                    pe.wait_ge(S["beta_ready"], 1)
                    t_.transpose(bank[3][:, 0:P], beta, ident).then_inc(S["betaT_done"], 1)
                if t in PRELUDE:
                    if t == 3:
                        pe.wait_ge(S["betaT_ready"], 1)
                    if t == 4:
                        pe.wait_ge(S["deT_lo"], 1)
                    gate_or_up(*PRELUDE[t])
                if t == 3:
                    pe.wait_ge(S["rdecT_ready"], 1)
                    pe.wait_ge(S["deT_lo"], KC)
                    t_.transpose(bank[5][:, 0:P], decT, ident).then_inc(S["rdec_done"], 1)
                    pe.wait_ge(S["consts_in"], 48)
                    for hg in range(HG):
                        mm = t_.matmul(bank[5][:, P + hg * NT:P + (hg + 1) * NT], con("headrows")[:, hg * P:(hg + 1) * P], endcol[:], start=True, stop=True)
                    mm.then_inc(S["enddec_done"], 1)

            def down_embed_products(v, beside=None):
                e, half = v % EC, v // EC
                n = h_place(v)
                wait_place_free(pe, n)
                if v == 0:
                    pe.wait_ge(S["deT_lo"], KC)
                product(place_bank(n)[:], [(lambda s, k=k: deT[:, s, k, e * P:(e + 1) * P], lambda s, k=k: xnT[:, s, k, half * HT:(half + 1) * HT])
                                           for k in range(KC)], beside).then_inc(S["h_done"], 1)

            def transpose_round(c, r):
                pe.wait_ge(S["tok_lo"], 4 * c + 2 * (r // 2) + 2)
                if c == 0 and r == 0:
                    pe.wait_ge(S["rdec_ready"], 1)
                    pe.wait_ge(S["enddec_ready"], 1)
                if r % 2 == 1:
                    pe.wait_ge(S["t_ready_act"], 2 * c + r // 2 + 1)
                elif c >= 1 or r >= 2:
                    pe.wait_ge(S["t_ready_dve"], 2 * c + r // 2)
                for which in range(2):
                    for i in range(2):
                        h = 4 * r + 2 * i
                        mm = t_.matmul(bank[5][:, (2 * which + i) * P:(2 * which + i + 1) * P],
                                       qk_tok[:, which, h:h + 2, :, :].rearrange("p h s d -> p (h s d)"), identr[:], start=True, stop=True)
                mm.then_inc(S["t_done"], 1)

            def scores(c, unit):
                pe.wait_ge(S["t_ready_act"], 2 * c + unit + 1)
                pe.wait_ge(S["t_ready_dve"], 2 * c + unit + 1)
                n = 2 * c + unit
                if n >= 1:
                    pe.wait_ge(S["sc_ready"], 2 * n)
                else:
                    pe.wait_ge(S["silu_ready"], 1)
                    pe.wait_ge(S["mlp_ready"], 1)
                for i in range(4):
                    for odd in range(2):
                        rws = slice(64 * odd, 64 * odd + 64)
                        mm = t_.matmul(bank[3 + odd][:, i * P:(i + 1) * P], qk4[rws, 2 * unit + i // 2, 1, i % 2, :],
                                       qk4[rws, 2 * unit + i // 2, 0, i % 2, :], start=True, stop=True)
                        if i == 3:
                            mm.then_inc(S["s_done"], 1)

            def chunk_update(c):
                if c == 0:
                    pe.wait_ge(S["ropeAB_ready"], 2 * NT)
                else:
                    pe.wait_ge(S["y_ready"], c)
                for hg in range(HG):
                    mm = t_.matmul(bank[6][:, hg * HPG * E1:(hg + 1) * HPG * E1], phi[:, c, HID + hg * P:HID + (hg + 1) * P],
                                   v1[:, c, hg * HPG:(hg + 1) * HPG, :].rearrange("p h e -> p (h e)"), start=True, stop=True)
                mm.then_inc(S["u_done"], 1)

            def q_transposes(c):
                pe.wait_ge(S["yT_lo"], c)
                if c >= 2:
                    pe.wait_ge(S["y_done"], c)
                for k in range(HG):
                    mm = t_.transpose(bank[7][:, k * P:(k + 1) * P], phi[:, c, k * P:(k + 1) * P], ident)
                mm.then_inc(S["qT_done"], 1)

            def y_transposes(c):
                pe.wait_ge(S["y_ready"], c + 1)
                if c >= 1:
                    pe.wait_ge(S["qT_ready"], c)
                for k in range(HG):
                    mm = t_.transpose(bank[7][:, k * P:(k + 1) * P], y[:, k * HPG:(k + 1) * HPG, :].rearrange("p h d -> p (h d)"), ident)
                mm.then_inc(S["yT_done"], 1)

            def outputs(c, part):
                if part == 0:
                    if c >= 1:
                        pe.wait_ge(S["y_ready"], c)
                    pe.wait_ge(S["upd_ready"], 2 * min(c + 1, NT - 1))
                    pe.wait_ge(S["sc_ready"], 4 * c + 2)
                if part == 2 and c >= 1:
                    pe.wait_ge(S["state_ready"], 2 * c)
                    pe.wait_ge(S["qT_ready"], c)
                    for hg in range(HG):
                        t_.matmul(bank[6][:, hg * HPG * E1:(hg + 1) * HPG * E1], qT[:, hg, :], state[:, hg, :], start=False, stop=False, skip_group_check=True)
                if part == 3:
                    pe.wait_ge(S["sc_ready"], 4 * c + 4)
                if part != 2:
                    quarter = part if part < 2 else part - 1
                    for h in range(4 * quarter, 4 * quarter + 4):
                        unit, i, odd = h // HPG, (h % HPG) // 2, h % 2
                        mm = t_.matmul(bank[6][:, h * E1:(h + 1) * E1], sc[:, unit, odd, i, :], v1[:, c, h, :],
                                       start=h == 0, stop=h == HEADS - 1, skip_group_check=True)
                    if part == 4:
                        mm.then_inc(S["y_done"], 1)

            def outputs_at(H, q):
                def beside(i):
                    for c, step in steps(H, q):
                        if step == 4 and i in (1, 3):
                            outputs(c, i // 2)
                        if step == 5 and i in (1, 2, 4):
                            outputs(c, (1, 2, 4).index(i) + 2)
                return beside

            def prob_transposes(g):
                pe.wait_ge(S["prob_ready"], g + 1)
                pe.wait_ge(S["beyond2_ready"], g // GPH + 1)
                if g % GPH >= 2:
                    pe.wait_ge(S["coefprod_ready"], g - 1)
                elif g % GPH == 0:
                    pe.wait_ge(S["sc_ready"], 4 * CPH * (g // GPH + 1))
                for e in range(EC):
                    mm = t_.transpose(bank[3 + g % 2][:, e * P:(e + 1) * P], prob[:, g % GPH, 2 * e:2 * e + 2, :].rearrange("p i j -> p (i j)"), ident)
                mm.then_inc(S["pT_done"], 1)

            def attention(H, q):
                for c, step in steps(H, q):
                    if step == 4:
                        scores(c, 1)
                        if c >= 1:
                            q_transposes(c)
                    if step == 6:
                        y_transposes(c)
                for c, step in steps(H, q):
                    if step in (0, 1, 3):
                        transpose_round(c, step)
                    if step == 2:
                        scores(c, 0)
                        transpose_round(c, 2)
                        if c < NT - 1:
                            chunk_update(c)

            transpose_round(0, 0)
            for H in range(HALVES):
                for q in range(START[0] if H == 0 else 0, PIECES):
                    beside = outputs_at(H, q)
                    if q < 2 * MC:
                        u = H * MC + q // 2
                        if q % 2 == 0:
                            gate_or_up(u, gate_p, gate_place(u), "gate_done", beside)
                        else:
                            gate_or_up(u, up_p, gate_place(u) + 1, "up_done", beside)
                    else:
                        down_embed_products(H * EC + q - 2 * MC, beside)
                    if (H, q) != (0, START[0]):
                        attention(H, q)
                for g in range(H * GPH, (H + 1) * GPH):
                    n = fin_place(g)
                    o = place_bank(n)[:, 0:HID]
                    wait_place_free(pe, n)
                    pe.wait_ge(S["act_lo"], (H + 1) * MC)
                    gc = group_cols(g, HT)
                    if g == 0:
                        for w in (-2, -1):
                            wait_split(pe, len(staged) + w)
                    first = g == H * GPH
                    for m in range(MC):
                        for i, (a, b) in enumerate(PASSES):
                            t_.matmul(o, act_p[:, a, m, gc], down_p[:, b, m, :], start=(m, i) == (0, 0), stop=False)
                            if first and H == 0 and i == 1 and m in (0, 1, 4, 5, 6):
                                outputs(CPH - 1, (0, 1, 4, 5, 6).index(m))
                        if first and m == 2:
                            attention(H, PIECES)
                        if m == (5, 3)[H]:
                            if first:
                                prob_transposes(g)
                            if g + 1 < (H + 1) * GPH:
                                prob_transposes(g + 1)
                    attention(H, PIECES + g % GPH + 1)
                    pe.wait_ge(S["yT_lo"], 2 * (g // 2) + 2)
                    for k in range(HG):
                        for a, b in PASSES:
                            t_.matmul(o, yT[:, a, k, gc], wo_p[:, b, k, :], start=False, stop=False)
                    pe.wait_ge(S["coef_lo"], g + 1)
                    for e in range(EC):
                        for a, b in PASSES:
                            mm = t_.matmul(o, coef[:, g % 2, a, e, :], ue_p[:, b, e, :], start=False, stop=e == EC - 1 and (a, b) == PASSES[-1])
                    mm.then_inc(S["fin_done"], 1)

        @block.vector
        def _(dve):
            v = nc.vector
            def statistics(T):
                dve.wait_ge(S[f"x{T}_in"], 16)
                for g in (2 * T, 2 * T + 1):
                    v.bn_stats(stats[:, g, :], x_sb[:, g, :]).then_inc(S["stat_ready"], 1)
                for g in (2 * T, 2 * T + 1):
                    dve.wait_ge(S["stat_ready"], g + 1)
                    v.bn_aggr(mv[:, g, :], stats[:, g, :]).then_inc(S["aggr_ready"], 1)
                dve.wait_ge(S["aggr_ready"], 2 * T + 2)
                v.tensor_scalar(std[:, 2 * T:2 * T + 2], mv[:, 2 * T:2 * T + 2, 1], EPS_LN, None, ALU.add).then_inc(S["std_in"], 1)

            def xnT_lo(g):
                dve.wait_ge(S["xnT_hi"], g + 1)
                gc = group_cols(g)
                v.tensor_tensor(xnT[:, LO, :, gc], bank[g % 3][:, 0:2 * P].rearrange("p (k n) -> p k n", k=KC), xnT[:, HI, :, gc].bitcast(F32),
                                ALU.subtract).then_inc(S["xnT_lo"], 1)

            def qrT_lo(half):
                dve.wait_ge(S["qrT_hi"], half + 1)
                v.tensor_tensor(qrT[:, LO, half * 512:half * 512 + 512], bank[3 + half][:], qrT[:, HI, half * 512:half * 512 + 512].bitcast(F32),
                                ALU.subtract).then_inc(S["qrT_lo"], 1)

            statistics(0)
            statistics(1)
            for T in range(NG // 2):
                dve.wait_ge(S["std_ready"], T + 1)
                v.reciprocal(rstd[:, 2 * T:2 * T + 2], std[:, 2 * T:2 * T + 2]).then_inc(S["rstd_ready"], 1)
                dve.wait_ge(S["rstd_ready"], T + 1)
                for g in (2 * T, 2 * T + 1):
                    if g >= 2:
                        dve.wait_ge(S["xnT_done"], g - 1)
                    v.tensor_scalar(xn[:, g % 2, :], x_sb[:, g, :], mv[:, g, 0:1], rstd[:, g:g + 1], ALU.subtract, ALU.mult).then_inc(S["xn_ready"], 1)
                    if g >= 2:
                        xnT_lo(g - 2)
                if T + 2 < NG // 2:
                    statistics(T + 2)
            xnT_lo(NG - 2)
            xnT_lo(NG - 1)
            dve.wait_ge(S["early_hi"], 2)
            at = slice(early_at(WQK), N_EARLY)
            v.tensor_tensor(early_p[:, LO, at], early[:, at], early_p[:, HI, at].bitcast(F32), ALU.subtract).then_inc(S["qk_w_lo"], 1)
            qrT_lo(0)
            qrT_lo(1)
            dve.wait_ge(S["consts_in"], 48)
            for dst, src in ((keyno[:].rearrange("p j b -> p (j b)"), "keyno"), (rankweight[:], "rankweight"), (causal[:], "causal"), (headblock[:], "headblock")):
                v.tensor_copy(dst, con(src)).then_inc(S["bf_consts"], 1)
            split_weights(dve, v, 1)
            for side in range(2):
                dve.wait_ge(S["route_ready"], side + 1)
                for g in range(NG):
                    v.max(top[:, side, g, :], route[:, side, g, :]).then_inc(S["top_ready"], 1)
                for g in range(NG):
                    dve.wait_ge(S["top_ready"], NG * side + g + 1)
                    v.max_index(topi[:, side, g, :], top[:, side, g, :], route[:, side, g, :]).then_inc(S["topi_ready"], 1)
            dve.wait_ge(S["z_ready"], NT)
            dve.wait_ge(S["bg_in"], 16)
            b3 = beta.rearrange("p (t h) -> p t h", h=HEADS)
            v.tensor_tensor(b3, b3, bg_sb[:].unsqueeze(1).broadcast_to([P, NT, HEADS]), ALU.add).then_inc(S["zb_ready"], 1)
            def rope(t):
                dve.wait_ge(S["qk_done"], t + 1)
                if t >= ROPES:
                    dve.wait_ge(S["phi_ready"], t - ROPES + 1)
                if t == NT - 3:
                    dve.wait_ge(S["enddec_done"], 1)
                b = bank[6 + t % 2][:].rearrange("p (h d) -> p h d", d=D)
                for z, w in ((ropeA[:, t % ROPES], "cos"), (phi[:, t], "sin")):
                    v.tensor_tensor(z.rearrange("p (h d) -> p h d", d=D), b,
                                    con(w)[:, t * D:(t + 1) * D].unsqueeze(1).broadcast_to([P, 2 * HEADS, D]), ALU.mult).then_inc(S["ropeAB_ready"], 1)

            def feature(t):
                dve.wait_ge(S["feat_in"], 2 * t + 2)
                v.scalar_tensor_tensor(phi[:, t, :], ropeA[:, t % ROPES], 1.0, phi[:, t], ALU.min, ALU.add).then_inc(S["phi_ready"], 1)

            def mlp(u):
                dve.wait_ge(S["silu_ready"], u + 1)
                dve.wait_ge(S["up_done"], u + 1)
                v.tensor_tensor(sil[:, u % 2], sil[:, u % 2], place_bank(gate_place(u) + 1)[:], ALU.mult).then_inc(S["mlp_ready"], 1)

            def choose_pairs():
                dve.wait_ge(S["pair_ready"], 1)
                for g in range(NG):
                    v.max(pair8[:, g, :], pair[:, g, :]).then_inc(S["pair8_ready"], 1)
                for g in range(NG):
                    dve.wait_ge(S["pair8_ready"], g + 1)
                    v.match_replace(chosen[:, g, :], pair8[:, g, :], pair[:, g, :], MARK).then_inc(S["marked_ready"], 1)
                dve.wait_ge(S["topi_ready"], 2 * NG)
                v.tensor_copy(xi[:], topi[:, 0]).then_inc(S["xi_ready"], 1)
                v.tensor_copy(yi[:], topi[:, 1]).then_inc(S["xi_ready"], 1)

            def count_pairs():
                dve.wait_ge(S["marked_ready"], NG)
                v.tensor_scalar(chosen, chosen, MARK, None, ALU.is_equal).then_inc(S["chosen_ready"], 1)
                dve.wait_ge(S["chosen_ready"], 1)
                v.tensor_reduce(rowcount[:], chosen.rearrange("p g (a b) -> p g a b", b=TOPK), AX.X, ALU.add).then_inc(S["rowcount_ready"], 1)

            def match_x():
                dve.wait_ge(S["xi_ready"], 1)
                dve.wait_ge(S["phi_ready"], NT)
                v.tensor_tensor(xmatch, xi[:].unsqueeze(2).broadcast_to([P, NG, NXI, TOPK]),
                                con("xno").rearrange("p (i a) -> p i a", a=TOPK).unsqueeze(1).broadcast_to([P, NG, NXI, TOPK]), ALU.is_equal).then_inc(S["xmatch_ready"], 1)

            for t in range(NT):
                if t == 4:
                    dve.wait_ge(S["rdec_done"], 1)
                    dve.wait_ge(S["enddec_done"], 1)
                    v.tensor_copy(rdec[:].rearrange("p t h -> p (t h)"), bank[5][:, 0:P]).then_inc(S["rdec_ready"], 1)
                    v.tensor_copy(enddec[:].rearrange("p k t -> p (k t)"), bank[5][:, P:P + HG * NT]).then_inc(S["enddec_ready"], 1)
                rope(t)
                if t == 0:
                    dve.wait_ge(S["zexp_ready"], 1)
                    v.tensor_scalar(beta, beta, 1.0, None, ALU.add).then_inc(S["zden_ready"], 1)
                    dve.wait_ge(S["zden_ready"], 1)
                    v.reciprocal(beta, beta).then_inc(S["zrec_ready"], 1)
                    dve.wait_ge(S["zrec_ready"], 1)
                    v.tensor_scalar(beta, beta, BETA_MIN, BETA_MAX, ALU.max, ALU.min).then_inc(S["beta_ready"], 1)
                if t == 2:
                    dve.wait_ge(S["betaT_done"], 1)
                    v.tensor_copy(betaT, bank[3][:, 0:P]).then_inc(S["betaT_ready"], 1)
                    dve.wait_ge(S["betaT_ready"], 1)
                    v.tensor_tensor_scan(decT, betaT, betaT, 1.0, ALU.mult, ALU.min).then_inc(S["decT_ready"], 1)
                    dve.wait_ge(S["decT_ready"], 1)
                    v.tensor_scalar(endcol[:], con("chunkcol"), decT[:, P - 1:P], None, ALU.mult).then_inc(S["endcol_ready"], 1)
                    dve.wait_ge(S["endcol_ready"], 1)
                    v.reciprocal(decT, decT).then_inc(S["rdecT_ready"], 1)
                if t == 1:
                    for k in range(KC):
                        dve.wait_ge(S["deT_hi"], k + 1)
                        v.tensor_tensor(deT[:, LO, k], bank[(4, 5)[k]][:], deT[:, HI, k].bitcast(F32), ALU.subtract).then_inc(S["deT_lo"], 1)
                if t == 2:
                    split_weights(dve, v, 3)
                if t >= 2:
                    feature(t - 2)
            feature(NT - 2)
            choose_pairs()
            mlp(0)
            mlp(1)
            feature(NT - 1)

            def rank_y(n):
                gs = slice(n * RANKED, (n + 1) * RANKED)
                if n == 0:
                    dve.wait_ge(S["bf_consts"], 4)
                    dve.wait_ge(S["xi_ready"], 2)
                else:
                    dve.wait_ge(S["yrank_steps"], 4 * n)
                v.tensor_tensor(ymatch, yi[:, gs, :].unsqueeze(2).broadcast_to([P, RANKED, NKEY, TOPK]),
                                keyno[:].unsqueeze(1).broadcast_to([P, RANKED, NKEY, TOPK]), ALU.is_equal).then_inc(S["ymatch_ready"], 1)
                dve.wait_ge(S["ymatch_ready"], n + 1)
                ym = ymatch.rearrange("p g j b -> p (g j) b")
                v.tensor_tensor(ym, ym, rankweight[:].unsqueeze(1).broadcast_to([P, RANKED * NKEY, TOPK]), ALU.mult).then_inc(S["yrank_steps"], 1)
                dve.wait_ge(S["yrank_steps"], 4 * n + 1)
                y4 = yt4.rearrange("p g j b -> p (g j) b")
                v.tensor_tensor(y4, ym[:, :, 0:4], ym[:, :, 4:8], ALU.add).then_inc(S["yrank_steps"], 1)
                dve.wait_ge(S["yrank_steps"], 4 * n + 2)
                v.tensor_tensor(ym[:, :, 0:2], y4[:, :, 0:2], y4[:, :, 2:4], ALU.add).then_inc(S["yrank_steps"], 1)
                dve.wait_ge(S["yrank_steps"], 4 * n + 3)
                v.tensor_tensor(yrank[:, gs, :].rearrange("p g j -> p (g j)"), ym[:, :, 0], ym[:, :, 1], ALU.add).then_inc(S["yrank_steps"], 1)

            def sums():
                dve.wait_ge(S["psel_ready"], 1)
                v.tensor_reduce(rowsum[:], pair.rearrange("p g (a b) -> p g a b", b=TOPK), AX.X, ALU.add).then_inc(S["rowsum_ready"], 1)
                dve.wait_ge(S["rowsum_ready"], 1)
                v.tensor_reduce(total[:], rowsum[:], AX.X, ALU.add).then_inc(S["total_ready"], 1)
                dve.wait_ge(S["total_ready"], 1)
                v.scalar_tensor_tensor(beyond[:], xi[:], float(NXI), rowsum[:], ALU.is_ge, ALU.mult).then_inc(S["beyond_ready"], 1)
                v.reciprocal(rtotal[:], total[:]).then_inc(S["rtotal_ready"], 1)
                dve.wait_ge(S["beyond_ready"], 1)
                v.tensor_reduce(beyond1[:], beyond[:], AX.X, ALU.add).then_inc(S["beyond1_ready"], 1)
                dve.wait_ge(S["xmatchc_ready"], 1)
                v.tensor_reduce(xcount[:], xmatch, AX.X, ALU.add).then_inc(S["xcount_ready"], 1)
                dve.wait_ge(S["xcount_ready"], 1)
                v.tensor_scalar(xcount[:], xcount[:], -1.0, float(TOPK), ALU.mult, ALU.add).then_inc(S["xlimit_ready"], 1)
                dve.wait_ge(S["rtotal_ready"], 1)
                dve.wait_ge(S["beyond1_ready"], 1)
                v.tensor_tensor(beyond1[:], beyond1[:], rtotal[:], ALU.mult).then_inc(S["beyond1_ready"], 1)

            def prob_mask(g):
                dve.wait_ge(S["xlimit_ready"], 1)
                dve.wait_ge(S["yrank_steps"], 4 * (g // RANKED + 1))
                if g < GPH:
                    for w in (-2, -1):
                        wait_split(dve, len(staged) + w)
                else:
                    dve.wait_ge(S["pT_done"], g - GPH + 1)
                v.tensor_tensor(prob[:, g % GPH], yrank[:, g].unsqueeze(1).broadcast_to([P, NXI, NKEY]),
                                xcount[:, g].unsqueeze(2).broadcast_to([P, NXI, NKEY]), ALU.is_gt).then_inc(S["prob0_ready"], 1)

            def copy_round(c, r):
                dve.wait_ge(S["t_done"], 4 * c + r + 1)
                if c >= 1:
                    dve.wait_ge(S["s_done"], 4 * (c - 1) + 2 * (r // 2) + 2)
                v.tensor_copy(qk4[:, r], bank[5][:].rearrange("p (w i n) -> p w i n", w=2, i=2)).then_inc(S["t_ready_dve"], 1)

            def mask(c, unit):
                if unit == 0 and c >= 1:
                    dve.wait_ge(S["y_done"], c)
                for odd in range(2):
                    dve.wait_ge(S["s_done"], 4 * c + 2 * unit + odd + 1)
                    v.tensor_tensor(sc[:, unit, odd], bank[3 + odd][:].rearrange("p (i n) -> p i n", n=P),
                                    causal[:].unsqueeze(1).broadcast_to([P, 4, P]), ALU.mult).then_inc(S["sc_ready"], 1)

            def chunk_sum(c):
                dve.wait_ge(S["u_done"], c + 1)
                dve.wait_ge(S["enddec_ready"], 1)
                if c >= 1:
                    dve.wait_ge(S["state_ready"], 2 * c)
                for hg in range(HG):
                    v.scalar_tensor_tensor(upd[:, hg], bank[6][:, hg * HPG * E1:(hg + 1) * HPG * E1], enddec[:, hg, c:c + 1],
                                           headblock[:], ALU.mult, ALU.mult).then_inc(S["upd_ready"], 1)

            def advance_state(c):
                for hg in range(HG):
                    dve.wait_ge(S["upd_ready"], 2 * c + hg + 1)
                    if c == 0:
                        v.tensor_copy(state[:, hg], upd[:, hg]).then_inc(S["state_ready"], 1)
                    else:
                        v.scalar_tensor_tensor(state[:, hg], state[:, hg], enddec[:, hg, c:c + 1], upd[:, hg], ALU.mult, ALU.add).then_inc(S["state_ready"], 1)

            def normalise(c):
                yb = bank[6][:, 0:HEADS * E1].rearrange("p (h e) -> p h e", e=E1)
                dve.wait_ge(S["y_done"], c + 1)
                v.scalar_tensor_tensor(den[:], rdec[:, c, :], EPS_DEN, yb[:, :, D], ALU.mult, ALU.add).then_inc(S["den_ready"], 1)
                dve.wait_ge(S["den_ready"], c + 1)
                v.reciprocal(rden[:], den[:]).then_inc(S["rden_ready"], 1)
                dve.wait_ge(S["rden_ready"], c + 1)
                if c == 0:
                    dve.wait_ge(S["psel_ready"], 1)
                if c >= 1:
                    dve.wait_ge(S["yT_done"], c)
                v.tensor_tensor(y, yb[:, :, 0:D], rden[:].unsqueeze(2).broadcast_to([P, HEADS, D]), ALU.mult).then_inc(S["y_ready"], 1)

            def yT_lo(c):
                dve.wait_ge(S["yT_hi"], c + 1)
                at = (c % CPH) * P
                v.tensor_tensor(yT[:, LO, :, at:at + P], bank[7][:, 0:HID].rearrange("p (k n) -> p k n", k=HG), yT[:, HI, :, at:at + P].bitcast(F32),
                                ALU.subtract).then_inc(S["yT_lo"], 1)

            def finish(g):
                dve.wait_ge(S["fin_done"], g + 1)
                dve.wait_ge(S["xb_ready"], g // 2 + 1)
                v.tensor_tensor(fin[:, g], place_bank(fin_place(g))[:, 0:HID], fin[:, g], ALU.add).then_inc(S["fin_ready"], 1)

            def coef_product(g):
                dve.wait_ge(S["pT_done"], g + 1)
                dve.wait_ge(S["h_ready"], (g // GPH + 1) * EC)
                hg_ = hT[:, :, group_cols(g, HT)]
                v.tensor_tensor(hg_, bank[3 + g % 2][:].rearrange("p (e n) -> p e n", n=P), hg_, ALU.mult).then_inc(S["coefprod_ready"], 1)

            def coef_lo(g):
                dve.wait_ge(S["coef_hi"], g + 1)
                if g % GPH >= 2:
                    dve.wait_ge(S["fin_done"], g - 1)
                v.tensor_tensor(coef[:, g % 2, LO], hT[:, :, group_cols(g, HT)], coef[:, g % 2, HI].bitcast(F32), ALU.subtract).then_inc(S["coef_lo"], 1)

            def attention(H, q):
                for c, step in steps(H, q):
                    if step == 4:
                        mask(c, 1)
                    if step == 5:
                        normalise(c)
                    if step == 6:
                        yT_lo(c)
                for c, step in steps(H, q):
                    if step == 1:
                        copy_round(c, 1)
                    if step == 3:
                        copy_round(c, 3)
                    if step == 2:
                        mask(c, 0)
                        if c < NT - 1:
                            chunk_sum(c)
                for c, step in steps(H, q):
                    if step == 5 and c < NT - 1:
                        advance_state(c)

            for H in range(HALVES):
                for q in range(START[0] if H == 0 else 0, PIECES):
                    if H == 0:
                        if q in (9, 13, 16, 17):
                            rank_y((9, 13, 16, 17).index(q))
                    attention(H, q)
                    if q < 2 * MC and q % 2 == 1:
                        mlp(H * MC + q // 2)
                    if H == 0:
                        if q == 5:
                            count_pairs()
                        if q == 5:
                            match_x()
                        if q in (6, 11):
                            split_weights(dve, v, 4 if q == 6 else 6)
                        if q == 10:
                            sums()
                        if q in (13, 14, 15, 18):
                            prob_mask((13, 14, 15, 18).index(q))
                    elif q in (2, 4, 6, 8):
                        prob_mask(GPH + q // 2 - 1)
                if H == 0:
                    attention(H, PIECES)
                dve.wait_ge(S["prob_ready"], (H + 1) * GPH)
                dve.wait_ge(S["beyond1_ready"], 2)
                v.tensor_tensor(prob[:, :, NXI - 1, NKEY - 1], prob[:, :, NXI - 1, NKEY - 1], beyond1[:, H * GPH:(H + 1) * GPH], ALU.add).then_inc(S["beyond2_ready"], 1)
                if H == 1:
                    attention(H, PIECES)
                coef_product(H * GPH)
                for g in range(H * GPH, (H + 1) * GPH):
                    coef_lo(g)
                    if g + 1 < (H + 1) * GPH:
                        coef_product(g + 1)
                    attention(H, PIECES + g % GPH + 1)
                    finish(g)


def constants():
    import numpy as np
    cols, n = const_columns()
    c = np.zeros((P, n), np.float32)

    def put(name, a):
        lo, hi = cols[name]
        c[:, lo:hi] = np.broadcast_to(np.asarray(a, np.float32).reshape(-1 if np.ndim(a) == 1 else P, *([] if np.ndim(a) == 1 else [-1])), (P, hi - lo))

    p = np.arange(P)
    put("ident", np.eye(P))
    put("causal", p[:, None] <= p[None, :])
    put("headblock", np.repeat(p[:, None] // D == np.arange(HPG)[None], E1, axis=1))
    half = D // 2
    inv_freq = np.float32(1.0) / np.float32(10000.0) ** (np.arange(half, dtype=np.float32) / np.float32(half))
    token = (np.arange(NT)[None, :] * P + p[:, None]).astype(np.float32) % np.float32(N_TOK)
    freqs = token[:, :, None] * inv_freq.astype(np.float32)
    put("cos", np.concatenate([np.cos(freqs)] * 2, axis=2).reshape(P, -1))
    put("sin", np.concatenate([np.sin(freqs), -np.sin(freqs)], axis=2).reshape(P, -1))
    put("keyno", np.repeat(np.arange(NKEY), TOPK))
    put("rankweight", TOPK - np.arange(TOPK))
    put("xno", np.repeat(np.arange(NXI), TOPK))
    put("chunkcol", p[:, None] // HEADS == np.arange(NT)[None])
    put("headrows", (p[:, None] % HEADS == (np.arange(HEADS).repeat(D))[None]))
    return c


_INS = ["L0_attn_x", "L0_attn_Wq", "L0_attn_Wk", "L0_attn_Wv", "L0_attn_Wg", "L0_attn_bg", "L0_attn_Wo", "L0_attn_bo",
        "L0_ffn_W_q", "L0_ffn_keys", "L0_ffn_down_embed", "L0_ffn_up_embed", "L0_ffn_gate_w", "L0_ffn_up_w", "L0_ffn_down_w"]


def kernel(**inputs):
    import numpy as np
    import concourse.bacc as bacc
    from concourse.bass_utils import run_bass_kernel_spmd

    nc = bacc.Bacc("TRN2", target_bir_lowering=False, num_devices=1)
    arrays, args = {}, []
    for name in _INS:
        a = np.ascontiguousarray(inputs[name])
        arrays[name] = a
        args.append(nc.dram_tensor(name, a.shape, mybir.dt.from_np(a.dtype), kind="ExternalInput").ap())
    arrays["constants"] = constants()
    args.append(nc.dram_tensor("constants", arrays["constants"].shape, F32, kind="ExternalInput").ap())
    out = nc.dram_tensor("out", (1, N_TOK, HID), F32, kind="ExternalOutput").ap()
    build(nc, *args, out)
    r = run_bass_kernel_spmd(nc, [arrays], core_ids=[0])
    return r.results[0]["out"]
```
